# Optimizing a Trainium2 kernel written in Bass

```python
import numpy as np
import jax
import jax.numpy as jnp

def _softmax(x, axis=-1):
    return jax.nn.softmax(x, axis=axis)

def _gelu(x):
    return jax.nn.gelu(x, approximate=True)

def _silu(x):
    return jax.nn.silu(x)

def _sigmoid(x):
    return jax.nn.sigmoid(x)

def _layernorm(x, axis=-1, eps=1e-05):
    m = jnp.mean(x, axis=axis, keepdims=True)
    v = jnp.var(x, axis=axis, keepdims=True)
    return (x - m) / jnp.sqrt(v + eps)

def _scatter_add(tgt, idx, src, axis=0):
    return tgt.at[idx].add(src)

def _segment_sum(src, seg, n):
    return jax.ops.segment_sum(src, seg, n)
kernel_name = 'mk_adj_resnorm_d1_adj_r2_368dfd'

def setup_inputs(seed: int=0):
    np.random.seed(seed)
    _w = jnp.asarray

    def _rec_inputs():
        import jax
        import jax.numpy as jnp
        _gk = jax.random.key(seed)
        x = -0.0005963 + 1.001 * jax.random.normal(jax.random.fold_in(_gk, 1), (2048, 256), jnp.float32)
        _a = jax.random.bernoulli(jax.random.fold_in(_gk, 2), 0.0078125, (2048, 2048))
        _a = jnp.logical_or(_a, jnp.swapaxes(_a, -1, -2))
        _a = jnp.logical_or(_a, jnp.eye(2048, dtype=bool))
        _af = _a.astype(jnp.float32)
        adj = _af
        return (x, adj)
    x, adj = _rec_inputs()

    def _L0_gnn_setup():
        import jax, jax.numpy as jnp
        import numpy as np
        N = 3072
        D_IN = 256
        D_OUT = 256
        DENSITY = 0.005
        key = jax.random.key(seed)
        ks = jax.random.split(key, 12)
        x = jax.random.normal(ks[0], (N, D_IN), dtype=jnp.float32)
        adj_a = (jax.random.uniform(ks[1], (N, N)) < DENSITY).astype(jnp.float32)
        adj_b = (jax.random.uniform(ks[2], (N, N)) < DENSITY).astype(jnp.float32)
        W_sa = jax.random.normal(ks[3], (D_IN, D_OUT), dtype=jnp.float32) * (1.414 / np.sqrt(D_IN + D_OUT))
        a_sa = jax.random.normal(ks[4], (1, 2 * D_OUT), dtype=jnp.float32) * (1.414 / np.sqrt(1 + 2 * D_OUT))
        stdv = 1.0 / np.sqrt(D_OUT)
        W_gcnb = jax.random.uniform(ks[5], (D_IN, D_OUT), minval=-stdv, maxval=stdv, dtype=jnp.float32)
        b_gcnb = jax.random.uniform(ks[6], (D_OUT,), minval=-stdv, maxval=stdv, dtype=jnp.float32)
        s = 1.0 / np.sqrt(2 * D_IN)
        Wa = jax.random.uniform(ks[7], (1, 2 * D_IN), minval=-s, maxval=s, dtype=jnp.float32)
        ba = jax.random.uniform(ks[8], (1,), minval=-s, maxval=s, dtype=jnp.float32)
        Wb = jax.random.uniform(ks[9], (1, 2 * D_IN), minval=-s, maxval=s, dtype=jnp.float32)
        bb = jax.random.uniform(ks[10], (1,), minval=-s, maxval=s, dtype=jnp.float32)
        return {'x': x, 'adj_a': adj_a, 'adj_b': adj_b, 'W_sa': W_sa, 'a_sa': a_sa, 'W_gcnb': W_gcnb, 'b_gcnb': b_gcnb, 'Wa': Wa, 'ba': ba, 'Wb': Wb, 'bb': bb}
    _L0_gnn_all = _L0_gnn_setup()
    _L0_gnn_in = {k: v for k, v in _L0_gnn_all.items() if k in ('W_sa', 'a_sa', 'W_gcnb', 'b_gcnb', 'Wa', 'ba', 'Wb', 'bb')}
    del _L0_gnn_all
    return {'x': x, 'adj': adj, 'L0_gnn_W_sa': _L0_gnn_in['W_sa'], 'L0_gnn_a_sa': _L0_gnn_in['a_sa'], 'L0_gnn_W_gcnb': _L0_gnn_in['W_gcnb'], 'L0_gnn_b_gcnb': _L0_gnn_in['b_gcnb'], 'L0_gnn_Wa': _L0_gnn_in['Wa'], 'L0_gnn_ba': _L0_gnn_in['ba'], 'L0_gnn_Wb': _L0_gnn_in['Wb'], 'L0_gnn_bb': _L0_gnn_in['bb']}

def reference(x, adj, L0_gnn_W_sa, L0_gnn_a_sa, L0_gnn_W_gcnb, L0_gnn_b_gcnb, L0_gnn_Wa, L0_gnn_ba, L0_gnn_Wb, L0_gnn_bb):
    import jax
    import jax.numpy as jnp

    def _L0_gnn_ref(x, adj_a, adj_b, W_sa, a_sa, W_gcnb, b_gcnb, Wa, ba, Wb, bb):
        import jax, jax.numpy as jnp
        import numpy as np
        N = 3072
        D_IN = 256
        D_OUT = 256
        DENSITY = 0.005
        type_sum_a = adj_a @ x
        type_sum_b = adj_b @ x
        attn_a = jax.nn.sigmoid(jnp.concatenate([type_sum_a, x], axis=1) @ Wa.T + ba)
        attn_b = jax.nn.sigmoid(jnp.concatenate([type_sum_b, x], axis=1) @ Wb.T + bb)
        h = x @ W_sa
        Hd = h.shape[1]
        s_left = h @ a_sa[0, :Hd]
        s_right = h @ a_sa[0, Hd:]
        scores = s_left[:, None] + s_right[None, :]
        e = jnp.where(adj_a != 0, jnp.exp(-jax.nn.leaky_relu(scores, 0.01)), 0.0)
        attn = e / (jnp.sum(e, axis=1, keepdims=True) + 1e-05)
        x_a = attn @ h
        x_b = adj_b @ (x @ W_gcnb) + b_gcnb
        return jax.nn.sigmoid(attn_a * x_a + attn_b * x_b)
    x = _layernorm(x + _L0_gnn_ref(x, adj, adj, L0_gnn_W_sa, L0_gnn_a_sa, L0_gnn_W_gcnb, L0_gnn_b_gcnb, L0_gnn_Wa, L0_gnn_ba, L0_gnn_Wb, L0_gnn_bb), axis=-1)
    return x

_drawn_inputs = setup_inputs


def setup_inputs(seed=0):
    import zlib

    import numpy as np

    out = dict(_drawn_inputs(seed))
    spreads = {}
    factors = {'L0_gnn_a_sa': 5.401, 'L0_gnn_b_gcnb': 8.0, 'L0_gnn_Wa': 4.394}
    for name, (base, spread) in spreads.items():
        noise = np.random.default_rng([zlib.crc32(name.encode()), seed]).standard_normal(out[name].shape)
        drawn = base * np.exp(spread * noise) if base else spread * noise
        out[name] = jnp.asarray(drawn.astype(out[name].dtype))
    for name, factor in factors.items():
        out[name] = (out[name] * factor).astype(out[name].dtype)
    return out
```

```python
from contextlib import ExitStack
import math

import concourse.bass as bass
from concourse import mybir

F32 = mybir.dt.float32
F16 = mybir.dt.float16
BF16 = mybir.dt.bfloat16
ALU = mybir.AluOpType
ACT = mybir.ActivationFunctionType
AX = mybir.AxisListType
MAXABS = bass.bass_isa.ReduceOp.absmax
MAX = bass.bass_isa.ReduceOp.max

P = 128
N = 2048
D = 256
KT = D // P
JT = N // P
IB = 512
NB = N // IB
IT = IB // P
GJ = 4
NG = JT // GJ
RC = 2 * D + 4
HC = D + 1
G0 = D + 2
GC = D + 2
ST = 8
SF = 4
LEAK = 0.01
EPS_SUM = 1e-5
EPS_VAR = 1e-5
FSHIFT = 14 * math.log(2.0)
XTOP = 2.0 ** 14
RDOWN = 2.0 ** -21
BIG = 1e30
TINY = 1e-30
UNSCALE = 1.0 / (XTOP * XTOP * RDOWN)


def graph_layer(nc, xT, xrows, adjT, w_rhs, w_small, w_saT, a_cols, b_row, gate_bias, expo, out):
    with ExitStack() as ctx:
        def sb(name, shape, dt):
            return ctx.enter_context(nc.sbuf_tensor(name, shape, dt))

        def psum(name):
            return ctx.enter_context(nc.psum_tensor(name, [P, 512], F32))

        def sem(name):
            return ctx.enter_context(nc.semaphore(name))

        x_t = sb("x_t", [P, KT, N], F32)
        x_parts = sb("x_parts", [P, 2, KT * N], F16)
        x_hi, x_lo = x_parts[:, 0, :], x_parts[:, 1, :]
        w_f = sb("w_f", [P, KT, 2 * D], F32)
        w_hi = sb("w_hi", [P, KT, 2 * D], F16)
        w_lo = sb("w_lo", [P, KT, 2 * D], F16)
        w6 = sb("w6", [P, KT, 6], F32)
        wsat = sb("wsat", [P, KT, D], F32)
        acols = sb("acols", [P, KT, 2], F32)
        ones = sb("ones", [P, P], F32)
        vl_wide = sb("vl_wide", [P, KT, P], F32)
        peaks = sb("peaks", [P, 4], F32)
        peaks_w = sb("peaks_w", [P, 2], F32)
        top = sb("top", [P, 2], F32)
        scale = sb("scale", [P, 2], F32)
        inv = sb("inv", [P, 2], F32)
        unscale = sb("unscale", [P, 1], F32)
        rscale = sb("rscale", [P, 1], F32)
        s6 = sb("s6", [P, JT, 6], F32)
        nsr = sb("nsr", [P, JT], F32)
        nsr_top = sb("nsr_top", [P, 1], F32)
        shift = sb("shift", [P, 1], F32)
        expo_f = sb("expo_f", [P, JT], F32)
        expo_q = sb("expo_q", [P, 1], F32)
        q = sb("q", [P, JT], F32)
        q_un = sb("q_un", [P, JT], F32)
        zc = sb("zc", [P, JT, 2], F32)
        zbias = sb("zbias", [P, 2], F32)
        bg = sb("bg", [P, D], F32)
        halfpow = sb("halfpow", [P, IT], F32)
        u_f = sb("u_f", [P, JT, 2], F32)
        sl_wide = sb("sl_wide", [P, N], F32)
        adj = sb("adj", [P, NB * JT * IB], F16)
        miss = sb("miss", [P, 2, GJ * IB], BF16)
        relu_s = sb("relu_s", [P, SF, IB], F32)
        f_32 = sb("f_32", [P, SF, IB], F32)
        f_hi = sb("f_hi", [P, ST, IB], F16)
        f_lo = sb("f_lo", [P, ST, IB], F16)
        r_hi = sb("r_hi", [P, JT, RC], F16)
        r_lo = sb("r_lo", [P, JT, RC], F16)
        x_r = sb("x_r", [P, JT, D], F32)
        mix_a, mix_b, mix_c, th = (x_t[:, k, h * IT * D:(h + 1) * IT * D].rearrange("p (t d) -> p t d", t=IT)
                                   for k in range(KT) for h in range(2))
        late = x_parts[:].rearrange("p a b -> p (a b)").bitcast(F32)
        res = late[:, 0:IT * D].rearrange("p (t d) -> p t d", t=IT)
        att_s = late[:, IT * D:IT * (D + GC)].rearrange("p (t d) -> p t d", t=IT)
        gcn_s = late[:, IT * (D + GC):IT * (D + 2 * GC)].rearrange("p (t d) -> p t d", t=IT)
        z = sb("z", [P, IT, 2], F32)
        th_z = sb("th_z", [P, IT, 2], F32)
        gate = sb("gate", [P, IT, 2], F32)
        den = sb("den", [P, IT], F32)
        rden = sb("rden", [P, IT], F32)
        alpha = sb("alpha", [P, IT], F32)
        alpha2 = sb("alpha2", [P, IT], F32)
        beta = sb("beta", [P, IT], F32)
        stats = sb("stats", [P, IT, 6], F32)
        mean2 = sb("mean2", [P, IT], F32)
        spread = sb("spread", [P, IT], F32)
        diff = sb("diff", [P, IT], F32)
        diff2 = sb("diff2", [P, IT], F32)
        mean = sb("mean", [P, IT], F32)
        var_in = sb("var_in", [P, IT], F32)
        var_eps = sb("var_eps", [P, IT], F32)
        rstd = sb("rstd", [P, IT], F32)

        att = [psum(f"att{i}") for i in range(IT)]
        gcn = [psum(f"gcn{i}") for i in range(IT)]

        small_loaded = sem("small_loaded")
        x_loaded = sem("x_loaded")
        rows_loaded = sem("rows_loaded")
        adj_dma = [sem(f"adj_dma{i}") for i in range(4)]
        adj_ready = sem("adj_ready")
        ones_set = sem("ones_set")
        v_done = sem("v_done")
        v_copied = sem("v_copied")
        vl_set = sem("vl_set")
        s6_done = sem("s6_done")
        s6_copied = sem("s6_copied")
        sl_done = sem("sl_done")
        sl_copied = sem("sl_copied")
        peaks_done = sem("peaks_done")
        top_done = sem("top_done")
        dve_step = sem("dve_step")
        scale_set = sem("scale_set")
        nsr_top_done = sem("nsr_top_done")
        shift_done = sem("shift_done")
        expo_set = sem("expo_set")
        q_done = sem("q_done")
        wh_done = sem("wh_done")
        w_split = sem("w_split")
        xh_done = sem("xh_done")
        xl_done = sem("xl_done")
        r_done = sem("r_done")
        rh_done = sem("rh_done")
        rl_done = sem("rl_done")
        r_cols = sem("r_cols")
        miss_set = sem("miss_set")
        relu_done = sem("relu_done")
        f32_done = sem("f32_done")
        fh_done = sem("fh_done")
        fl_done = sem("fl_done")
        unit_used = sem("unit_used")
        att_out = sem("att_out")
        gcn_out = sem("gcn_out")
        z_set = sem("z_set")
        thz_done = sem("thz_done")
        alpha_set = sem("alpha_set")
        mixa_done = sem("mixa_done")
        mixc_done = sem("mixc_done")
        th_done = sem("th_done")
        var_set = sem("var_set")
        rstd_done = sem("rstd_done")
        half_added = sem("half_added")
        mixb_done = sem("mixb_done")
        res_done = sem("res_done")
        stats_done = sem("stats_done")
        res_out = sem("res_out")
        stored = sem("stored")

        block = ctx.enter_context(nc.Block())

        PRE = 8

        @block.sync
        def _(sp):
            sp.dma_start(wsat[:], w_saT).then_inc(small_loaded, 16)
            sp.dma_start(acols[:], a_cols).then_inc(small_loaded, 16)
            sp.dma_start(w6[:, :, 0:4], w_small).then_inc(small_loaded, 16)
            for c in range(NB):
                sp.dma_start(x_t[:, :, c * IB:(c + 1) * IB], xT[:, :, c * IB:(c + 1) * IB]).then_inc(x_loaded, 16)
            sp.dma_start(w_f[:], w_rhs).then_inc(small_loaded, 16)
            sp.dma_start(bg[:], b_row.partition_broadcast(P)).then_inc(small_loaded, 16)
            sp.dma_start(zbias[:], gate_bias.partition_broadcast(P)).then_inc(small_loaded, 16)
            sp.dma_start(halfpow[:], expo.partition_broadcast(P)).then_inc(small_loaded, 16)
            sp.dma_start(x_r[:], xrows).then_inc(rows_loaded, 16)
            with sp.Fori(0, NB) as b:
                sp.wait_ge(res_out, b * IT + IT)
                sp.dma_start(out[:, bass.ds(b * IT, IT), :],
                             x_r[:, bass.ds(b * IT, IT), :]).then_inc(stored, 16)
            sp.wait_ge(stored, NB * 16)

        @block.gpsimd
        def _(pool):
            def load_adj(n):
                pool.dma_start(adj[:, n * GJ * IB:(n + 1) * GJ * IB],
                               adjT[:, n * GJ * IB:(n + 1) * GJ * IB]).then_inc(adj_dma[n % 4], 16)

            for n in range(4):
                load_adj(n)
            pool.wait_ge(peaks_done, 1)
            nc.gpsimd.partition_all_reduce(top[:], peaks_w[:], P, MAXABS).then_inc(top_done, 1)
            pool.wait_ge(nsr_top_done, 1)
            nc.gpsimd.partition_all_reduce(shift[:], nsr_top[:], P, MAX).then_inc(shift_done, 1)
            for n in range(4, NB * NG):
                pool.wait_ge(adj_dma[n % 4], 16 * (n // 4))
                pool.sem_inc(adj_ready, 1)
                load_adj(n)
            for n in range(NB * NG, NB * NG + 4):
                pool.wait_ge(adj_dma[n % 4], 16 * (n // 4))
                pool.sem_inc(adj_ready, 1)
            pool.wait_ge(small_loaded, 16 * 7)
            with pool.Fori(0, NB) as b:
                pool.wait_ge(var_set, b + 1)
                nc.gpsimd.tensor_tensor(rstd[:], var_eps[:], halfpow[:], ALU.pow).then_inc(rstd_done, 1)

        @block.scalar
        def _(act):
            def exp_f(n, jt):
                act.wait_ge(relu_done, n + 1)
                if not isinstance(n, int) or n >= SF:
                    act.wait_ge(fl_done, n - SF + 1)
                nc.scalar.activation(f_32[:, jt % SF, :], relu_s[:, jt % SF, :], ACT.Exp,
                                     bias=expo_f[:, jt:jt + 1], scale=-(1.0 - LEAK)).then_inc(f32_done, 1)

            def cast_f(n, jt):
                act.wait_ge(f32_done, n + 1)
                if not isinstance(n, int) or n >= ST:
                    act.wait_ge(unit_used, n - ST + 1)
                nc.scalar.copy(f_hi[:, jt % ST, :], f_32[:, jt % SF, :]).then_inc(fh_done, 1)

            def step(n, jt):
                exp_f(n, jt)
                if not isinstance(n, int) or n >= 1:
                    cast_f(n - 1, (jt - 1) % JT)

            act.wait_ge(small_loaded, 16 * 7)
            act.wait_ge(v_done, 1)
            for k in range(KT):
                ins = nc.scalar.copy(w6[:, k, 4:6], gcn[0][:, 2 * k:2 * k + 2])
            ins.then_inc(v_copied, 1)
            act.wait_ge(s6_done, 1)
            nc.scalar.copy(s6[:], gcn[1][:, 0:JT * 6]).then_inc(s6_copied, 1)
            for c in range(NB):
                act.wait_ge(sl_done, c + 1)
                nc.scalar.copy(sl_wide[:, c * IB:(c + 1) * IB], att[c][:]).then_inc(sl_copied, 1)
            act.wait_ge(scale_set, 1)
            for k in range(KT):
                nc.scalar.activation(w_hi[:, k, :], w_f[:, k, :], ACT.Copy,
                                     scale=scale[:, 1:2]).then_inc(wh_done, 1)
            for c in range(NB):
                nc.scalar.activation(x_hi.rearrange("p (k i) -> p k i", k=KT)[:, :, c * IB:(c + 1) * IB],
                                     x_t[:, :, c * IB:(c + 1) * IB], ACT.Copy,
                                     scale=scale[:, 0:1]).then_inc(xh_done, 1)
            act.wait_ge(expo_set, 1)
            nc.scalar.activation(q[:], s6[:, :, 4], ACT.Exp, bias=expo_q[:], scale=-LEAK).then_inc(q_done, 1)
            for t in range(JT):
                act.wait_ge(r_done, t + 1)
                nc.scalar.activation(
                    r_hi[:, t, 0:2 * G0].rearrange("p (h d) -> p h d", h=2)[:, :, 0:D],
                    att[t % IT][:].rearrange("p (h d) -> p h d", h=2), ACT.Copy, scale=RDOWN).then_inc(rh_done, 1)
                if t % 2 == 1:
                    step(t // 2, t // 2)
            for n in range(PRE, JT):
                step(n, n)

            def att_copy(b):
                for it in range(IT):
                    act.wait_ge(unit_used, b * JT + JT)
                    nc.scalar.copy(att_s[:, it, 0:HC], att[it][:, 0:HC]).then_inc(att_out, 1)

            def tanh_gates(b):
                act.wait_ge(z_set, b + 1)
                nc.scalar.activation(th_z[:], z[:], ACT.Tanh, scale=0.5).then_inc(thz_done, 1)

            def scale_att(b, it):
                act.wait_ge(alpha_set, b + 1)
                nc.scalar.activation(mix_a[:, it, :], att_s[:, it, 0:D], ACT.Copy,
                                     scale=alpha2[:, it:it + 1]).then_inc(mixa_done, 1)

            def tanh_mix(b, it):
                act.wait_ge(mixc_done, b * IT + it + 1)
                nc.scalar.activation(th[:, it, :], mix_c[:, it, :], ACT.Tanh, scale=0.5).then_inc(th_done, 1)

            with act.Fori(1, NB) as b:
                for u in range(JT):
                    step(b * JT + u, u)
                    if u == 3:
                        att_copy(b - 1)
                    if u == 4:
                        tanh_gates(b - 1)
                    if u >= 6 and u % 2 == 0 and (u - 6) // 2 < IT:
                        scale_att(b - 1, (u - 6) // 2)
                    if u >= 7 and u % 2 == 1 and (u - 7) // 2 < IT:
                        tanh_mix(b - 1, (u - 7) // 2)
            cast_f(NB * JT - 1, JT - 1)
            att_copy(NB - 1)
            tanh_gates(NB - 1)
            for it in range(IT):
                scale_att(NB - 1, it)
            for it in range(IT):
                tanh_mix(NB - 1, it)

        @block.vector
        def _(dve):
            chain = [0]

            def link(ins):
                chain[0] += 1
                ins.then_inc(dve_step, 1)
                dve.wait_ge(dve_step, chain[0])

            def missing(b, g):
                dve.wait_ge(adj_ready, b * NG + g + 1)
                nc.vector.tensor_scalar(miss[:, g % 2, :], adj[:, bass.ds((b * NG + g) * GJ * IB, GJ * IB)],
                                        0.0, BIG, ALU.is_equal, ALU.mult).then_inc(miss_set, 1)

            def masked_relu(n, b, jt):
                dve.wait_ge(miss_set, b * NG + jt // GJ + 1)
                if not isinstance(n, int) or n >= SF:
                    dve.wait_ge(f32_done, n - SF + 1)
                nc.vector.scalar_tensor_tensor(
                    out=relu_s[:, jt % SF, :], in0=sl_wide[:, bass.ds(b * IB, IB)], scalar=s6[:, jt, 5:6],
                    in1=miss[:, (jt // GJ) % 2, (jt % GJ) * IB:(jt % GJ + 1) * IB],
                    op0=ALU.add, op1=ALU.max).then_inc(relu_done, 1)

            def low_part(n, jt):
                dve.wait_ge(fh_done, n + 1)
                if not isinstance(n, int) or n >= ST:
                    dve.wait_ge(unit_used, n - ST + 1)
                nc.vector.tensor_tensor(f_lo[:, jt % ST, :], f_32[:, jt % SF, :], f_hi[:, jt % ST, :],
                                        ALU.subtract).then_inc(fl_done, 1)

            def step(n, b, jt):
                if jt % GJ == 0:
                    missing(b, jt // GJ)
                masked_relu(n, b, jt)
                if not isinstance(n, int) or n >= 2:
                    low_part(n - 2, (jt - 2) % JT)

            nc.vector.memset(ones[:], 1.0).then_inc(ones_set, 1)
            nc.vector.memset(r_hi[:, :, D:D + 2], 1.0).then_inc(r_cols, 1)
            nc.vector.memset(r_lo[:, :, D:D + 2], 0.0).then_inc(r_cols, 1)
            dve.wait_ge(ones_set, 1)
            dve.wait_ge(v_copied, 1)
            for k in range(KT):
                nc.vector.tensor_scalar(vl_wide[:, k, :], ones[:], w6[:, k, 4:5], None,
                                        ALU.mult).then_inc(vl_set, 1)
            dve.wait_ge(small_loaded, 16 * 7)
            nc.vector.tensor_reduce(peaks[:, 1:2], w_f[:], AX.XY, ALU.max, apply_absolute_value=True)
            link(nc.vector.tensor_reduce(peaks[:, 2:3], w6[:, :, 0:2], AX.XY, ALU.max, apply_absolute_value=True))
            nc.vector.tensor_tensor(peaks_w[:, 1:2], peaks[:, 1:2], peaks[:, 2:3], ALU.max)
            dve.wait_ge(x_loaded, 16 * NB)
            link(nc.vector.tensor_reduce(peaks_w[:, 0:1], x_t[:], AX.XY, ALU.max, apply_absolute_value=True))
            nc.vector.tensor_scalar(peaks_w[:], peaks_w[:], TINY, None, ALU.max).then_inc(peaks_done, 1)
            dve.wait_ge(s6_copied, 1)
            link(nc.vector.tensor_scalar(nsr[:], s6[:, :, 5], -LEAK, None, ALU.mult))
            nc.vector.tensor_reduce(nsr_top[:], nsr[:], AX.X, ALU.max).then_inc(nsr_top_done, 1)
            dve.wait_ge(top_done, 1)
            link(nc.vector.reciprocal(inv[:], top[:]))
            nc.vector.tensor_scalar(scale[:], inv[:], XTOP, None, ALU.mult).then_inc(scale_set, 1)
            nc.vector.tensor_scalar(unscale[:], top[:, 0:1], top[:, 1:2], UNSCALE, ALU.mult, ALU.mult)
            dve.wait_ge(scale_set, 1)
            link(nc.vector.tensor_scalar(rscale[:], scale[:, 0:1], scale[:, 1:2], RDOWN, ALU.mult, ALU.mult))
            dve.wait_ge(wh_done, KT)
            for k in range(KT):
                nc.vector.scalar_tensor_tensor(out=w_lo[:, k, :], in0=w_f[:, k, :], scalar=scale[:, 1:2],
                                               in1=w_hi[:, k, :], op0=ALU.mult,
                                               op1=ALU.subtract).then_inc(w_split, 1)

            def x_low(c):
                dve.wait_ge(xh_done, c + 1)
                nc.vector.scalar_tensor_tensor(
                    out=x_lo.rearrange("p (k i) -> p k i", k=KT)[:, :, c * IB:(c + 1) * IB],
                    in0=x_t[:, :, c * IB:(c + 1) * IB], scalar=scale[:, 0:1],
                    in1=x_hi.rearrange("p (k i) -> p k i", k=KT)[:, :, c * IB:(c + 1) * IB],
                    op0=ALU.mult, op1=ALU.subtract).then_inc(xl_done, 1)

            x_low(0)
            dve.wait_ge(shift_done, 1)
            nc.vector.tensor_scalar(expo_q[:], shift[:], -FSHIFT, None, ALU.add)
            nc.vector.tensor_scalar(expo_f[:], nsr[:], shift[:], FSHIFT, ALU.subtract, ALU.add)\
              .then_inc(expo_set, 1)
            x_low(1)
            link(nc.vector.tensor_scalar(u_f[:], s6[:, :, 0:2], rscale[:], None, ALU.mult))
            link(nc.vector.tensor_copy(r_hi[:, :, G0 + D:G0 + D + 2], u_f[:]))
            nc.vector.tensor_tensor(r_lo[:, :, G0 + D:G0 + D + 2], u_f[:], r_hi[:, :, G0 + D:G0 + D + 2],
                                    ALU.subtract).then_inc(r_cols, 1)
            for c in range(2):
                nc.vector.tensor_scalar(zc[:, :, c], s6[:, :, 2 + c], zbias[:, c:c + 1], None, ALU.add)
            x_low(2)
            x_low(3)
            dve.wait_ge(sl_copied, NB)
            for t in range(JT):
                dve.wait_ge(rh_done, t + 1)
                nc.vector.scalar_tensor_tensor(
                    out=r_lo[:, t, 0:2 * G0].rearrange("p (h d) -> p h d", h=2)[:, :, 0:D],
                    in0=att[t % IT][:].rearrange("p (h d) -> p h d", h=2), scalar=RDOWN,
                    in1=r_hi[:, t, 0:2 * G0].rearrange("p (h d) -> p h d", h=2)[:, :, 0:D],
                    op0=ALU.mult, op1=ALU.subtract).then_inc(rl_done, 1)
                if t % 2 == 1:
                    step(t // 2, 0, t // 2)
            dve.wait_ge(rows_loaded, 16)
            nc.vector.tensor_scalar(x_r[:], x_r[:], 0.5, None, ALU.add).then_inc(half_added, 1)
            dve.wait_ge(q_done, 1)
            nc.vector.tensor_scalar(q_un[:], q[:], unscale[:], None, ALU.mult)
            for n in range(PRE, JT):
                step(n, 0, n)

            base = chain[0]
            LINKS = 8

            def block_link(b, k, ins):
                ins.then_inc(dve_step, 1)
                dve.wait_ge(dve_step, base + b * LINKS + k + 1)

            def gcn_copy(b):
                for it in range(IT):
                    dve.wait_ge(unit_used, b * JT + JT)
                    nc.vector.tensor_copy(gcn_s[:, it, :], gcn[it][:, 0:GC]).then_inc(gcn_out, 1)

            def gates_in(b):
                dve.wait_ge(gcn_out, b * IT + IT)
                nc.vector.scalar_tensor_tensor(out=z[:], in0=gcn_s[:, :, D:D + 2], scalar=unscale[:],
                                               in1=zc[:, bass.ds(b * IT, IT), :], op0=ALU.mult,
                                               op1=ALU.add).then_inc(z_set, 1)
                dve.wait_ge(att_out, b * IT + IT)
                block_link(b, 0, nc.vector.tensor_tensor(den[:], att_s[:, :, D], q[:, bass.ds(b * IT, IT)],
                                                         ALU.mult))
                block_link(b, 1, nc.vector.tensor_scalar(den[:], den[:], EPS_SUM, None, ALU.add))
                block_link(b, 2, nc.vector.reciprocal(rden[:], den[:]))
                block_link(b, 3, nc.vector.tensor_tensor(alpha[:], rden[:], q_un[:, bass.ds(b * IT, IT)],
                                                         ALU.mult))

            def gates_out(b):
                dve.wait_ge(thz_done, b + 1)
                block_link(b, 4, nc.vector.tensor_scalar(gate[:], th_z[:], 0.5, 0.5, ALU.mult, ALU.add))
                nc.vector.tensor_tensor(alpha2[:], alpha[:], gate[:, :, 0], ALU.mult).then_inc(alpha_set, 1)
                block_link(b, 5, nc.vector.tensor_scalar(beta[:], gate[:, :, 1], unscale[:], None, ALU.mult))

            def mix(b, it):
                dve.wait_ge(mixa_done, b * IT + it + 1)
                nc.vector.scalar_tensor_tensor(out=mix_b[:, it, :], in0=gcn_s[:, it, 0:D],
                                               scalar=beta[:, it:it + 1], in1=mix_a[:, it, :],
                                               op0=ALU.mult, op1=ALU.add).then_inc(mixb_done, 1)
                dve.wait_ge(mixb_done, b * IT + it + 1)
                nc.vector.scalar_tensor_tensor(out=mix_c[:, it, :], in0=bg[:], scalar=gate[:, it, 1:2],
                                               in1=mix_b[:, it, :], op0=ALU.mult,
                                               op1=ALU.add).then_inc(mixc_done, 1)

            def residual(b, it):
                dve.wait_ge(th_done, b * IT + it + 1)
                nc.vector.scalar_tensor_tensor(out=res[:, it, :], in0=th[:, it, :], scalar=0.5,
                                               in1=x_r[:, bass.ds(b * IT + it, 1), :], op0=ALU.mult,
                                               op1=ALU.add).then_inc(res_done, 1)
                dve.wait_ge(res_done, b * IT + it + 1)
                nc.vector.bn_stats(stats[:, it, :], res[:, it, :]).then_inc(stats_done, 1)

            def variance(b):
                dve.wait_ge(stats_done, b * IT + IT)
                nc.vector.tensor_tensor(mean2[:], stats[:, :, 1], stats[:, :, 4], ALU.add)
                nc.vector.tensor_tensor(spread[:], stats[:, :, 2], stats[:, :, 5], ALU.add)
                block_link(b, 6, nc.vector.tensor_tensor(diff[:], stats[:, :, 1], stats[:, :, 4], ALU.subtract))
                nc.vector.tensor_scalar(mean[:], mean2[:], 0.5, None, ALU.mult)
                nc.vector.tensor_scalar(var_in[:], spread[:], 1.0 / D, EPS_VAR, ALU.mult, ALU.add)
                block_link(b, 7, nc.vector.tensor_tensor(diff2[:], diff[:], diff[:], ALU.mult))
                nc.vector.scalar_tensor_tensor(out=var_eps[:], in0=diff2[:], scalar=0.25, in1=var_in[:],
                                               op0=ALU.mult, op1=ALU.add).then_inc(var_set, 1)

            def normalise(b):
                dve.wait_ge(rstd_done, b + 1)
                for it in range(IT):
                    nc.vector.tensor_scalar(x_r[:, bass.ds(b * IT + it, 1), :], res[:, it, :],
                                            mean[:, it:it + 1], rstd[:, it:it + 1], ALU.subtract,
                                            ALU.mult).then_inc(res_out, 1)

            with dve.Fori(1, NB) as b:
                for u in range(JT):
                    step(b * JT + u, b, u)
                    if u == 3:
                        gcn_copy(b - 1)
                        gates_in(b - 1)
                    if u == 5:
                        gates_out(b - 1)
                    if u >= 7 and u % 2 == 1 and (u - 7) // 2 < IT:
                        mix(b - 1, (u - 7) // 2)
                    if u >= 8 and u % 2 == 0 and (u - 8) // 2 < IT:
                        residual(b - 1, (u - 8) // 2)
                    if u == JT - 2:
                        variance(b - 1)
                    if u == JT - 1:
                        normalise(b - 1)
            low_part(NB * JT - 2, JT - 2)
            low_part(NB * JT - 1, JT - 1)
            gcn_copy(NB - 1)
            gates_in(NB - 1)
            gates_out(NB - 1)
            for it in range(IT):
                mix(NB - 1, it)
            for it in range(IT):
                residual(NB - 1, it)
            variance(NB - 1)
            normalise(NB - 1)

        @block.tensor
        def _(pe):
            pe.wait_ge(small_loaded, 16 * 7)
            for k in range(KT):
                for dk in range(KT):
                    ins = nc.tensor.matmul(gcn[0][:, 2 * k:2 * k + 2], wsat[:, dk, k * P:(k + 1) * P],
                                           acols[:, dk, :], start=(dk == 0), stop=(dk == KT - 1))
            ins.then_inc(v_done, 1)
            pe.wait_ge(x_loaded, 16 * NB)
            pe.wait_ge(v_copied, 1)
            for t in range(JT):
                for k in range(KT):
                    ins = nc.tensor.matmul(gcn[1][:, 6 * t:6 * t + 6], x_t[:, k, t * P:(t + 1) * P],
                                           w6[:, k, :], start=(k == 0), stop=(k == KT - 1))
            ins.then_inc(s6_done, 1)
            pe.wait_ge(vl_set, KT)
            for c in range(NB):
                for k in range(KT):
                    ins = nc.tensor.matmul(att[c][:], vl_wide[:, k, :], x_t[:, k, c * IB:(c + 1) * IB],
                                           start=(k == 0), stop=(k == KT - 1))
                ins.then_inc(sl_done, 1)
            pe.wait_ge(w_split, KT)
            for t in range(JT):
                if t < IT:
                    pe.wait_ge(sl_copied, t + 1)
                else:
                    pe.wait_ge(rl_done, t - IT + 1)
                pe.wait_ge(xl_done, t // IT + 1)
                for k in range(KT):
                    xs = slice(k * N + t * P, k * N + (t + 1) * P)
                    for i, (xx, ww) in enumerate(((x_hi, w_hi), (x_hi, w_lo), (x_lo, w_hi))):
                        ins = nc.tensor.matmul(att[t % IT][:], xx[:, xs], ww[:, k, :],
                                               start=(k == 0 and i == 0), stop=(k == KT - 1 and i == 2))
                ins.then_inc(r_done, 1)
            pe.wait_ge(r_cols, 3)
            pe.wait_ge(rl_done, JT)
            pe.wait_ge(s6_copied, 1)

            def unit(b, jt):
                n = b * JT + jt
                first, last = jt == 0, jt == JT - 1
                if jt % GJ == 0:
                    pe.wait_ge(adj_ready, b * NG + jt // GJ + 1)
                for it in range(IT):
                    if first and not isinstance(b, int):
                        pe.wait_ge(gcn_out, (b - 1) * IT + it + 1)
                    a = adj[:, bass.ds((b * JT + jt) * IB + it * P, P)]
                    nc.tensor.matmul(gcn[it][:, 0:GC], a, r_hi[:, jt, G0:RC], start=first, stop=False,
                                     skip_group_check=True)
                    nc.tensor.matmul(gcn[it][:, 0:GC], a, r_lo[:, jt, G0:RC], start=False, stop=last,
                                     skip_group_check=True)
                pe.wait_ge(fh_done, n + 1)
                for it in range(IT):
                    if first and not isinstance(b, int):
                        pe.wait_ge(att_out, (b - 1) * IT + it + 1)
                    f = f_hi[:, jt % ST, it * P:(it + 1) * P]
                    nc.tensor.matmul(att[it][:, 0:HC], f, r_hi[:, jt, 0:HC], start=first, stop=False,
                                     skip_group_check=True)
                    nc.tensor.matmul(att[it][:, 0:HC], f, r_lo[:, jt, 0:HC], start=False, stop=False,
                                     skip_group_check=True)
                pe.wait_ge(fl_done, n + 1)
                for it in range(IT):
                    ins = nc.tensor.matmul(att[it][:, 0:HC], f_lo[:, jt % ST, it * P:(it + 1) * P],
                                           r_hi[:, jt, 0:HC], start=False, stop=last, skip_group_check=True)
                ins.then_inc(unit_used, 1)

            for jt in range(JT):
                unit(0, jt)
            with pe.Fori(1, NB) as b:
                for jt in range(JT):
                    unit(b, jt)


def kernel(x, adj, L0_gnn_W_sa, L0_gnn_a_sa, L0_gnn_W_gcnb, L0_gnn_b_gcnb, L0_gnn_Wa, L0_gnn_ba, L0_gnn_Wb,
           L0_gnn_bb):
    import numpy as np
    import concourse.bacc as bacc
    from concourse.bass_utils import run_bass_kernel_spmd

    x, adj = np.asarray(x), np.asarray(adj)
    w_sa, w_g = np.asarray(L0_gnn_W_sa), np.asarray(L0_gnn_W_gcnb)
    a_sa, wa, wb = np.asarray(L0_gnn_a_sa)[0], np.asarray(L0_gnn_Wa)[0], np.asarray(L0_gnn_Wb)[0]

    def rows(m):
        return np.ascontiguousarray(m.reshape(-1, P, m.shape[-1]).transpose(1, 0, 2))

    arrays = {
        "in_xT": rows(np.ascontiguousarray(x.T)),
        "in_xrows": rows(x),
        "in_adjT": np.ascontiguousarray(
            adj.T.reshape(JT, P, NB, IB).transpose(1, 2, 0, 3).reshape(P, NB * JT * IB)),
        "in_w": rows(np.concatenate([w_sa, w_g], axis=1)),
        "in_w_small": rows(np.stack([wa[:D], wb[:D], wa[D:], wb[D:]], axis=1)),
        "in_w_saT": rows(np.ascontiguousarray(w_sa.T)),
        "in_a_cols": rows(np.stack([a_sa[:D], a_sa[D:]], axis=1)),
        "in_b_row": np.ascontiguousarray(np.asarray(L0_gnn_b_gcnb)),
        "in_gate_bias": np.concatenate([np.asarray(L0_gnn_ba), np.asarray(L0_gnn_bb)]),
        "in_exponent": np.full((IT,), -0.5, np.float32),
    }
    nc = bacc.Bacc("TRN2", target_bir_lowering=False, num_devices=1)
    args = [nc.dram_tensor(name, a.shape, mybir.dt.from_np(a.dtype), kind="ExternalInput").ap()
            for name, a in arrays.items()]
    out = nc.dram_tensor("out_dram", (P, JT, D), F32, kind="ExternalOutput").ap()
    graph_layer(nc, *args, out)
    r = run_bass_kernel_spmd(nc, [arrays], core_ids=[0])
    got = r.results[0]["out_dram"]
    return np.ascontiguousarray(got.transpose(1, 0, 2).reshape(N, D))
```

```python
from contextlib import ExitStack
import math

import concourse.bass as bass
from concourse import mybir

F32 = mybir.dt.float32
F16 = mybir.dt.float16
BF16 = mybir.dt.bfloat16
ALU = mybir.AluOpType
ACT = mybir.ActivationFunctionType
AX = mybir.AxisListType
MAXABS = bass.bass_isa.ReduceOp.absmax
MAX = bass.bass_isa.ReduceOp.max

P = 128
N = 2048
D = 256
KT = D // P
JT = N // P
IB = 512
NB = N // IB
IT = IB // P
GJ = 4
NG = JT // GJ
RC = 2 * D + 4
HC = D + 1
G0 = D + 2
GC = D + 2
ST = 8
SF = 4
LEAK = 0.01
EPS_SUM = 1e-5
EPS_VAR = 1e-5
PRE = 4
FSHIFT = 14 * math.log(2.0)
XTOP = 2.0 ** 14
RDOWN = 2.0 ** -21
BIG = 1e30
TINY = 1e-30
UNSCALE = 1.0 / (XTOP * XTOP * RDOWN)


def graph_layer(nc, xT, xrows, adjT, w_rhs, w_small, w_saT, a_cols, b_row, gate_bias, expo, out):
    with ExitStack() as ctx:
        def sb(name, shape, dt):
            return ctx.enter_context(nc.sbuf_tensor(name, shape, dt))

        def psum(name):
            return ctx.enter_context(nc.psum_tensor(name, [P, 512], F32))

        def sem(name):
            return ctx.enter_context(nc.semaphore(name))

        x_t = sb("x_t", [P, KT, N], F32)
        x_parts = sb("x_parts", [P, 2, KT * N], F16)
        x_hi, x_lo = x_parts[:, 0, :], x_parts[:, 1, :]
        w_f = sb("w_f", [P, KT, 2 * D], F32)
        w_hi = sb("w_hi", [P, KT, 2 * D], F16)
        w_lo = sb("w_lo", [P, KT, 2 * D], F16)
        w6 = sb("w6", [P, KT, 6], F32)
        wsat = sb("wsat", [P, KT, D], F32)
        acols = sb("acols", [P, KT, 2], F32)
        ones = sb("ones", [P, P], F32)
        vl_wide = sb("vl_wide", [P, KT, P], F32)
        peaks = sb("peaks", [P, NB + 2], F32)
        peaks_m = sb("peaks_m", [P, 2], F32)
        peaks_w = sb("peaks_w", [P, 2], F32)
        top = sb("top", [P, 2], F32)
        scale = sb("scale", [P, 2], F32)
        inv = sb("inv", [P, 2], F32)
        unscale = sb("unscale", [P, 1], F32)
        rscale = sb("rscale", [P, 1], F32)
        s6 = sb("s6", [P, JT, 6], F32)
        nsr = sb("nsr", [P, JT], F32)
        nsr_top = sb("nsr_top", [P, 1], F32)
        shift = sb("shift", [P, 1], F32)
        expo_f = sb("expo_f", [P, JT], F32)
        expo_q = sb("expo_q", [P, 1], F32)
        q = sb("q", [P, JT], F32)
        q_un = sb("q_un", [P, JT], F32)
        zc = sb("zc", [P, JT, 2], F32)
        zbias = sb("zbias", [P, 2], F32)
        bg = sb("bg", [P, D], F32)
        halfpow = sb("halfpow", [P, IT], F32)
        u_f = sb("u_f", [P, JT, 2], F32)
        sl_wide = sb("sl_wide", [P, N], F32)
        adj = sb("adj", [P, NB * JT * IB], F16)
        miss = sb("miss", [P, 2, GJ * IB], BF16)
        relu_s = sb("relu_s", [P, SF, IB], F32)
        f_32 = sb("f_32", [P, SF, IB], F32)
        f_hi = sb("f_hi", [P, ST, IB], F16)
        f_lo = sb("f_lo", [P, ST, IB], F16)
        r_hi = sb("r_hi", [P, JT, RC], F16)
        r_lo = sb("r_lo", [P, JT, RC], F16)
        x_r = sb("x_r", [P, JT, D], F32)
        mix_a, mix_b, mix_c, th = (x_t[:, k, h * IT * D:(h + 1) * IT * D].rearrange("p (t d) -> p t d", t=IT)
                                   for k in range(KT) for h in range(2))
        late = x_parts[:].rearrange("p a b -> p (a b)").bitcast(F32)
        res = late[:, 0:IT * D].rearrange("p (t d) -> p t d", t=IT)
        att_s = late[:, IT * D:IT * (D + GC)].rearrange("p (t d) -> p t d", t=IT)
        gcn_s = late[:, IT * (D + GC):IT * (D + 2 * GC)].rearrange("p (t d) -> p t d", t=IT)
        z = sb("z", [P, IT, 2], F32)
        th_z = sb("th_z", [P, IT, 2], F32)
        gate = sb("gate", [P, IT, 2], F32)
        den = sb("den", [P, IT], F32)
        rden = sb("rden", [P, IT], F32)
        alpha = sb("alpha", [P, IT], F32)
        alpha2 = sb("alpha2", [P, IT], F32)
        beta = sb("beta", [P, IT], F32)
        stats = sb("stats", [P, IT, 6], F32)
        mean2 = sb("mean2", [P, IT], F32)
        spread = sb("spread", [P, IT], F32)
        diff = sb("diff", [P, IT], F32)
        diff2 = sb("diff2", [P, IT], F32)
        mean = sb("mean", [P, IT], F32)
        var_in = sb("var_in", [P, IT], F32)
        mv = sb("mv", [P, IT, 2], F32)
        var_eps = sb("var_eps", [P, IT], F32)
        rstd = sb("rstd", [P, IT], F32)

        att = [psum(f"att{i}") for i in range(IT)]
        gcn = [psum(f"gcn{i}") for i in range(IT)]

        v_loaded = sem("v_loaded")
        w_loaded = sem("w_loaded")
        misc_loaded = sem("misc_loaded")
        x_loaded = [sem(f"x_loaded{c}") for c in range(NB)]
        peak_parts = sem("peak_parts")
        rows_loaded = sem("rows_loaded")
        adj_dma = [sem(f"adj_dma{i}") for i in range(4)]
        adj_ready = sem("adj_ready")
        ones_set = sem("ones_set")
        v_done = sem("v_done")
        v_copied = sem("v_copied")
        vl_set = sem("vl_set")
        s6_done = sem("s6_done")
        s6_copied = sem("s6_copied")
        sl_done = sem("sl_done")
        sl_copied = sem("sl_copied")
        peaks_done = sem("peaks_done")
        top_done = sem("top_done")
        dve_step = sem("dve_step")
        scale_set = sem("scale_set")
        nsr_top_done = sem("nsr_top_done")
        shift_done = sem("shift_done")
        expo_set = sem("expo_set")
        q_done = sem("q_done")
        wh_done = sem("wh_done")
        w_split = sem("w_split")
        xh_done = sem("xh_done")
        xl_done = sem("xl_done")
        r_done = sem("r_done")
        rh_done = sem("rh_done")
        rl_done = sem("rl_done")
        r_cols = sem("r_cols")
        miss_set = sem("miss_set")
        relu_done = sem("relu_done")
        f32_done = sem("f32_done")
        fh_done = sem("fh_done")
        fl_done = sem("fl_done")
        sums_done = sem("sums_done")
        unit_used = sem("unit_used")
        att_out = sem("att_out")
        gcn_out = sem("gcn_out")
        z_set = sem("z_set")
        thz_done = sem("thz_done")
        gate_set = sem("gate_set")
        mixa_done = sem("mixa_done")
        mixc_done = sem("mixc_done")
        th_done = sem("th_done")
        var_set = sem("var_set")
        rstd_done = sem("rstd_done")
        half_added = sem("half_added")
        mixb_done = sem("mixb_done")
        res_done = sem("res_done")
        stats_done = sem("stats_done")
        res_out = sem("res_out")
        stored = sem("stored")

        block = ctx.enter_context(nc.Block())

        x_hi3 = x_hi.rearrange("p (k i) -> p k i", k=KT)
        x_lo3 = x_lo.rearrange("p (k i) -> p k i", k=KT)

        def halves(r, t):
            return r[:, t, 0:2 * G0].rearrange("p (h d) -> p h d", h=2)[:, :, 0:D]

        def wait_sums(eng, b, it):
            if it == IT - 1 and not isinstance(b, int):
                eng.wait_ge(unit_used, b * JT + JT)
            else:
                eng.wait_ge(sums_done, b * (IT - 1) + it + 1)

        @block.sync
        def _(sp):
            sp.dma_start(wsat[:], w_saT).then_inc(v_loaded, 16)
            sp.dma_start(acols[:], a_cols).then_inc(v_loaded, 16)
            sp.dma_start(w6[:, :, 0:4], w_small).then_inc(v_loaded, 16)
            for c in range(NB):
                sp.dma_start(x_t[:, :, c * IB:(c + 1) * IB], xT[:, :, c * IB:(c + 1) * IB]).then_inc(x_loaded[c], 16)
            sp.dma_start(w_f[:], w_rhs).then_inc(w_loaded, 16)
            sp.dma_start(zbias[:], gate_bias.partition_broadcast(P)).then_inc(misc_loaded, 16)
            sp.dma_start(bg[:], b_row.partition_broadcast(P)).then_inc(misc_loaded, 16)
            sp.dma_start(halfpow[:], expo.partition_broadcast(P)).then_inc(misc_loaded, 16)
            sp.wait_ge(adj_ready, 1)
            sp.dma_start(x_r[:], xrows).then_inc(rows_loaded, 16)
            with sp.Fori(0, NB - 1) as b:
                sp.wait_ge(res_out, b * IT + IT)
                sp.dma_start(out[:, bass.ds(b * IT, IT), :],
                             x_r[:, bass.ds(b * IT, IT), :]).then_inc(stored, 16)
            for m in range(JT - IT, JT):
                sp.wait_ge(res_out, m + 1)
                sp.dma_start(out[:, m, :], x_r[:, m, :]).then_inc(stored, 16)
            sp.wait_ge(stored, (NB - 1 + IT) * 16)

        @block.gpsimd
        def _(pool):
            def load_adj(n):
                pool.dma_start(adj[:, n * GJ * IB:(n + 1) * GJ * IB],
                               adjT[:, n * GJ * IB:(n + 1) * GJ * IB]).then_inc(adj_dma[n % 4], 16)

            def landed(n):
                pool.wait_ge(adj_dma[n % 4], 16 * (n // 4 + 1))
                pool.sem_inc(adj_ready, 1)

            pool.wait_ge(x_loaded[NB - 1], 16)
            load_adj(0)
            pool.wait_ge(peaks_done, 1)
            nc.gpsimd.partition_all_reduce(top[:], peaks_w[:], P, MAXABS).then_inc(top_done, 1)
            load_adj(1)
            landed(0)
            pool.wait_ge(nsr_top_done, 1)
            nc.gpsimd.partition_all_reduce(shift[:], nsr_top[:], P, MAX).then_inc(shift_done, 1)
            load_adj(2)
            load_adj(3)
            for n in range(4, NB * NG):
                load_adj(n)
                landed(n - 3)
            for n in range(NB * NG - 3, NB * NG):
                landed(n)
            pool.wait_ge(misc_loaded, 16 * 3)
            with pool.Fori(0, NB - 1) as b:
                pool.wait_ge(var_set, b + 1)
                nc.gpsimd.tensor_tensor(rstd[:], var_eps[:], halfpow[:], ALU.pow).then_inc(rstd_done, 1)
            for it in range(IT):
                pool.wait_ge(var_set, NB + it)
                nc.gpsimd.tensor_tensor(rstd[:, it:it + 1], var_eps[:, it:it + 1], halfpow[:, it:it + 1],
                                        ALU.pow).then_inc(rstd_done, 1)

        @block.scalar
        def _(act):
            def exp_f(n, jt):
                act.wait_ge(relu_done, n + 1)
                if not isinstance(n, int) or n >= SF:
                    act.wait_ge(fl_done, n - SF + 1)
                nc.scalar.activation(f_32[:, jt % SF, :], relu_s[:, jt % SF, :], ACT.Exp,
                                     bias=expo_f[:, jt:jt + 1], scale=-(1.0 - LEAK)).then_inc(f32_done, 1)

            def cast_f(n, jt):
                act.wait_ge(f32_done, n + 1)
                if not isinstance(n, int) or n >= ST:
                    act.wait_ge(unit_used, n - ST + 1)
                nc.scalar.copy(f_hi[:, jt % ST, :], f_32[:, jt % SF, :]).then_inc(fh_done, 1)

            def step(n, jt):
                exp_f(n, jt)
                if not isinstance(n, int) or n >= 1:
                    cast_f(n - 1, (jt - 1) % JT)

            def sl_copy(c):
                act.wait_ge(sl_done, c + 1)
                nc.scalar.copy(sl_wide[:, c * IB:(c + 1) * IB], att[c][:]).then_inc(sl_copied, 1)

            def x_high(c):
                nc.scalar.activation(x_hi3[:, :, c * IB:(c + 1) * IB], x_t[:, :, c * IB:(c + 1) * IB], ACT.Copy,
                                     scale=scale[:, 0:1]).then_inc(xh_done, 1)

            act.wait_ge(v_done, 1)
            nc.scalar.copy(w6[:, :, 4:6], gcn[0][:, 0:2 * KT].rearrange("p (k c) -> p k c", k=KT))\
              .then_inc(v_copied, 1)
            for c in range(NB - 1):
                sl_copy(c)
            act.wait_ge(scale_set, 1)
            for k in range(KT):
                nc.scalar.activation(w_hi[:, k, :], w_f[:, k, :], ACT.Copy,
                                     scale=scale[:, 1:2]).then_inc(wh_done, 1)
            x_high(0)
            act.wait_ge(s6_done, 1)
            nc.scalar.copy(s6[:], gcn[1][:, 0:JT * 6]).then_inc(s6_copied, 1)
            sl_copy(NB - 1)
            x_high(1)
            act.wait_ge(expo_set, 1)
            nc.scalar.activation(q[:], s6[:, :, 4], ACT.Exp, bias=expo_q[:], scale=-LEAK).then_inc(q_done, 1)
            for t in range(JT):
                act.wait_ge(r_done, t + 1)
                nc.scalar.activation(halves(r_hi, t), att[t % IT][:].rearrange("p (h d) -> p h d", h=2),
                                     ACT.Copy, scale=RDOWN).then_inc(rh_done, 1)
                if t == 0 or t == IT:
                    x_high(2 + t // IT)
                if t % IT == IT - 1:
                    step(t // IT, t // IT)
            for n in range(PRE, JT):
                step(n, n)
                if n % IT == 1:
                    g = n // IT - 1
                    act.wait_ge(rows_loaded, 16)
                    nc.scalar.activation(x_r[:, g * IT:(g + 1) * IT, :], x_r[:, g * IT:(g + 1) * IT, :],
                                         ACT.Copy, bias=0.5).then_inc(half_added, 1)

            def att_copy(b):
                for it in range(IT):
                    wait_sums(act, b, it)
                    nc.scalar.copy(att_s[:, it, 0:HC], att[it][:, 0:HC]).then_inc(att_out, 1)

            def tanh_gates(b):
                act.wait_ge(z_set, b + 1)
                nc.scalar.activation(th_z[:], z[:], ACT.Tanh, scale=0.5).then_inc(thz_done, 1)

            def gated_bias(it, gates):
                act.wait_ge(gate_set, gates)
                nc.scalar.activation(mix_a[:, it, :], bg[:], ACT.Copy,
                                     scale=gate[:, it, 1:2]).then_inc(mixa_done, 1)

            def tanh_mix(b, it):
                act.wait_ge(mixc_done, b * IT + it + 1)
                nc.scalar.activation(th[:, it, :], mix_c[:, it, :], ACT.Tanh, scale=0.5).then_inc(th_done, 1)

            act.wait_ge(misc_loaded, 16 * 3)
            with act.Fori(1, NB) as b:
                for u in range(JT):
                    step(b * JT + u, u)
                    if u == 3:
                        att_copy(b - 1)
                    if u == 4:
                        tanh_gates(b - 1)
                    if u >= 6 and u % 2 == 0 and (u - 6) // 2 < IT:
                        gated_bias((u - 6) // 2, b)
                    if u >= 7 and u % 2 == 1 and (u - 7) // 2 < IT:
                        tanh_mix(b - 1, (u - 7) // 2)
            cast_f(NB * JT - 1, JT - 1)
            for it in range(IT):
                act.wait_ge(z_set, NB + it)
                nc.scalar.activation(th_z[:, it, :], z[:, it, :], ACT.Tanh, scale=0.5).then_inc(thz_done, 1)
                gated_bias(it, NB + it)
                tanh_mix(NB - 1, it)

        @block.vector
        def _(dve):
            chain = [0]

            def link(ins):
                chain[0] += 1
                ins.then_inc(dve_step, 1)
                dve.wait_ge(dve_step, chain[0])

            def missing(b, g):
                dve.wait_ge(adj_ready, b * NG + g + 1)
                nc.vector.tensor_scalar(miss[:, g % 2, :], adj[:, bass.ds((b * NG + g) * GJ * IB, GJ * IB)],
                                        0.0, BIG, ALU.is_equal, ALU.mult).then_inc(miss_set, 1)

            def masked_relu(n, b, jt):
                dve.wait_ge(miss_set, b * NG + jt // GJ + 1)
                if not isinstance(n, int) or n >= SF:
                    dve.wait_ge(f32_done, n - SF + 1)
                nc.vector.scalar_tensor_tensor(
                    out=relu_s[:, jt % SF, :], in0=sl_wide[:, bass.ds(b * IB, IB)], scalar=s6[:, jt, 5:6],
                    in1=miss[:, (jt // GJ) % 2, (jt % GJ) * IB:(jt % GJ + 1) * IB],
                    op0=ALU.add, op1=ALU.max).then_inc(relu_done, 1)

            def low_part(n, jt):
                dve.wait_ge(fh_done, n + 1)
                if not isinstance(n, int) or n >= ST:
                    dve.wait_ge(unit_used, n - ST + 1)
                nc.vector.tensor_tensor(f_lo[:, jt % ST, :], f_32[:, jt % SF, :], f_hi[:, jt % ST, :],
                                        ALU.subtract).then_inc(fl_done, 1)

            def step(n, b, jt):
                if jt % GJ == 0:
                    missing(b, jt // GJ)
                masked_relu(n, b, jt)
                if not isinstance(n, int) or n >= 2:
                    low_part(n - 2, (jt - 2) % JT)

            def x_low(c):
                dve.wait_ge(xh_done, c + 1)
                nc.vector.scalar_tensor_tensor(
                    out=x_lo3[:, :, c * IB:(c + 1) * IB], in0=x_t[:, :, c * IB:(c + 1) * IB],
                    scalar=scale[:, 0:1], in1=x_hi3[:, :, c * IB:(c + 1) * IB],
                    op0=ALU.mult, op1=ALU.subtract).then_inc(xl_done, 1)

            nc.vector.memset(ones[:], 1.0).then_inc(ones_set, 1)
            nc.vector.memset(r_hi[:, :, D:D + 2], 1.0).then_inc(r_cols, 1)
            dve.wait_ge(ones_set, 1)
            dve.wait_ge(v_copied, 1)
            for k in range(KT):
                nc.vector.tensor_scalar(vl_wide[:, k, :], ones[:], w6[:, k, 4:5], None,
                                        ALU.mult).then_inc(vl_set, 1)
            for c in range(NB):
                dve.wait_ge(x_loaded[c], 16)
                nc.vector.tensor_reduce(peaks[:, c:c + 1], x_t[:, :, c * IB:(c + 1) * IB], AX.XY, ALU.max,
                                        apply_absolute_value=True).then_inc(peak_parts, 1)
            nc.vector.tensor_reduce(peaks[:, NB + 1:NB + 2], w6[:, :, 0:2], AX.XY, ALU.max,
                                    apply_absolute_value=True).then_inc(peak_parts, 1)
            dve.wait_ge(w_loaded, 16)
            nc.vector.tensor_reduce(peaks[:, NB:NB + 1], w_f[:], AX.XY, ALU.max,
                                    apply_absolute_value=True).then_inc(peak_parts, 1)
            dve.wait_ge(peak_parts, NB + 2)
            nc.vector.tensor_reduce(peaks_m[:, 0:1], peaks[:, 0:NB], AX.X, ALU.max)
            link(nc.vector.tensor_reduce(peaks_m[:, 1:2], peaks[:, NB:NB + 2], AX.X, ALU.max))
            nc.vector.tensor_scalar(peaks_w[:], peaks_m[:], TINY, None, ALU.max).then_inc(peaks_done, 1)
            dve.wait_ge(top_done, 1)
            link(nc.vector.reciprocal(inv[:], top[:]))
            nc.vector.tensor_scalar(scale[:], inv[:], XTOP, None, ALU.mult).then_inc(scale_set, 1)
            nc.vector.tensor_scalar(unscale[:], top[:, 0:1], top[:, 1:2], UNSCALE, ALU.mult, ALU.mult)
            dve.wait_ge(scale_set, 1)
            link(nc.vector.tensor_scalar(rscale[:], scale[:, 0:1], scale[:, 1:2], RDOWN, ALU.mult, ALU.mult))
            for k in range(KT):
                dve.wait_ge(wh_done, k + 1)
                nc.vector.scalar_tensor_tensor(out=w_lo[:, k, :], in0=w_f[:, k, :], scalar=scale[:, 1:2],
                                               in1=w_hi[:, k, :], op0=ALU.mult,
                                               op1=ALU.subtract).then_inc(w_split, 1)
            x_low(0)
            dve.wait_ge(s6_copied, 1)
            link(nc.vector.tensor_scalar(nsr[:], s6[:, :, 5], -LEAK, None, ALU.mult))
            nc.vector.tensor_reduce(nsr_top[:], nsr[:], AX.X, ALU.max).then_inc(nsr_top_done, 1)
            link(nc.vector.tensor_scalar(u_f[:], s6[:, :, 0:2], rscale[:], None, ALU.mult))
            link(nc.vector.tensor_copy(r_hi[:, :, G0 + D:G0 + D + 2], u_f[:]))
            nc.vector.tensor_tensor(r_lo[:, :, G0 + D:G0 + D + 2], u_f[:], r_hi[:, :, G0 + D:G0 + D + 2],
                                    ALU.subtract).then_inc(r_cols, 1)
            dve.wait_ge(misc_loaded, 16 * 3)
            for c in range(2):
                nc.vector.tensor_scalar(zc[:, :, c], s6[:, :, 2 + c], zbias[:, c:c + 1], None, ALU.add)
            dve.wait_ge(shift_done, 1)
            nc.vector.tensor_scalar(expo_q[:], shift[:], -FSHIFT, None, ALU.add)
            nc.vector.tensor_scalar(expo_f[:], nsr[:], shift[:], FSHIFT, ALU.subtract, ALU.add)\
              .then_inc(expo_set, 1)
            x_low(1)
            dve.wait_ge(sl_copied, NB)
            for t in range(JT):
                dve.wait_ge(rh_done, t + 1)
                nc.vector.scalar_tensor_tensor(
                    out=halves(r_lo, t), in0=att[t % IT][:].rearrange("p (h d) -> p h d", h=2), scalar=RDOWN,
                    in1=halves(r_hi, t), op0=ALU.mult, op1=ALU.subtract).then_inc(rl_done, 1)
                if t == 1 or t == 1 + IT:
                    x_low(2 + t // IT)
                if t % IT == IT - 1:
                    step(t // IT, 0, t // IT)
            dve.wait_ge(q_done, 1)
            nc.vector.tensor_scalar(q_un[:], q[:], unscale[:], None, ALU.mult)
            for n in range(PRE, JT):
                step(n, 0, n)

            base = chain[0]
            LINKS = 8

            def block_link(b, k, ins):
                ins.then_inc(dve_step, 1)
                dve.wait_ge(dve_step, base + b * LINKS + k + 1)

            def gcn_copy(b):
                for it in range(IT):
                    wait_sums(dve, b, it)
                    nc.vector.tensor_copy(gcn_s[:, it, :], gcn[it][:, 0:GC]).then_inc(gcn_out, 1)

            def gates_in(b):
                dve.wait_ge(gcn_out, (b + 1) * IT + IT)
                nc.vector.scalar_tensor_tensor(out=z[:], in0=gcn_s[:, :, D:D + 2], scalar=unscale[:],
                                               in1=zc[:, bass.ds(b * IT, IT), :], op0=ALU.mult,
                                               op1=ALU.add).then_inc(z_set, 1)
                dve.wait_ge(att_out, (b + 1) * IT + IT)
                block_link(b, 0, nc.vector.tensor_tensor(den[:], att_s[:, :, D], q[:, bass.ds(b * IT, IT)],
                                                         ALU.mult))
                block_link(b, 1, nc.vector.tensor_scalar(den[:], den[:], EPS_SUM, None, ALU.add))
                block_link(b, 2, nc.vector.reciprocal(rden[:], den[:]))
                block_link(b, 3, nc.vector.tensor_tensor(alpha[:], rden[:], q_un[:, bass.ds(b * IT, IT)],
                                                         ALU.mult))

            def gates_out(b):
                dve.wait_ge(thz_done, b + 1)
                nc.vector.tensor_scalar(gate[:], th_z[:], 0.5, 0.5, ALU.mult, ALU.add).then_inc(gate_set, 1)
                dve.wait_ge(gate_set, b + 1)
                nc.vector.tensor_scalar(beta[:], gate[:, :, 1], unscale[:], None, ALU.mult)
                block_link(b, 4, nc.vector.tensor_tensor(alpha2[:], alpha[:], gate[:, :, 0], ALU.mult))

            def mix(b, it, gcn_in, att_in):
                dve.wait_ge(mixa_done, b * IT + it + 1)
                nc.vector.scalar_tensor_tensor(out=mix_b[:, it, :], in0=gcn_in, scalar=beta[:, it:it + 1],
                                               in1=mix_a[:, it, :], op0=ALU.mult,
                                               op1=ALU.add).then_inc(mixb_done, 1)
                dve.wait_ge(mixb_done, b * IT + it + 1)
                nc.vector.scalar_tensor_tensor(out=mix_c[:, it, :], in0=att_in, scalar=alpha2[:, it:it + 1],
                                               in1=mix_b[:, it, :], op0=ALU.mult,
                                               op1=ALU.add).then_inc(mixc_done, 1)

            def residual(b, it):
                dve.wait_ge(th_done, b * IT + it + 1)
                nc.vector.scalar_tensor_tensor(out=res[:, it, :], in0=th[:, it, :], scalar=0.5,
                                               in1=x_r[:, bass.ds(b * IT + it, 1), :], op0=ALU.mult,
                                               op1=ALU.add).then_inc(res_done, 1)
                dve.wait_ge(res_done, b * IT + it + 1)
                nc.vector.bn_stats(stats[:, it, :], res[:, it, :]).then_inc(stats_done, 1)

            def variance(b):
                dve.wait_ge(stats_done, b * IT + IT)
                nc.vector.tensor_tensor(mean2[:], stats[:, :, 1], stats[:, :, 4], ALU.add)
                nc.vector.tensor_tensor(spread[:], stats[:, :, 2], stats[:, :, 5], ALU.add)
                block_link(b, 5, nc.vector.tensor_tensor(diff[:], stats[:, :, 1], stats[:, :, 4], ALU.subtract))
                nc.vector.tensor_scalar(mean[:], mean2[:], 0.5, None, ALU.mult)
                nc.vector.tensor_scalar(var_in[:], spread[:], 1.0 / D, EPS_VAR, ALU.mult, ALU.add)
                block_link(b, 6, nc.vector.tensor_tensor(diff2[:], diff[:], diff[:], ALU.mult))
                nc.vector.scalar_tensor_tensor(out=var_eps[:], in0=diff2[:], scalar=0.25, in1=var_in[:],
                                               op0=ALU.mult, op1=ALU.add).then_inc(var_set, 1)

            def normalise(b):
                dve.wait_ge(rstd_done, b + 1)
                for it in range(IT):
                    nc.vector.tensor_scalar(x_r[:, bass.ds(b * IT + it, 1), :], res[:, it, :],
                                            mean[:, it:it + 1], rstd[:, it:it + 1], ALU.subtract,
                                            ALU.mult).then_inc(res_out, 1)

            dve.wait_ge(half_added, IT - 1)
            with dve.Fori(1, NB) as b:
                for u in range(JT):
                    step(b * JT + u, b, u)
                    if u == 3:
                        gcn_copy(b - 1)
                        gates_in(b - 1)
                    if u == 5:
                        gates_out(b - 1)
                    if u >= 7 and u % 2 == 1 and (u - 7) // 2 < IT:
                        it = (u - 7) // 2
                        mix(b - 1, it, gcn_s[:, it, 0:D], att_s[:, it, 0:D])
                    if u >= 8 and u % 2 == 0 and (u - 8) // 2 < IT:
                        residual(b - 1, (u - 8) // 2)
                    if u == JT - 2:
                        variance(b - 1)
                    if u == JT - 1:
                        block_link(b - 1, 7, nc.vector.tensor_copy(mean2[:], mean[:]))
                        normalise(b - 1)
            low_part(NB * JT - 2, JT - 2)
            low_part(NB * JT - 1, JT - 1)

            chain[0] = base + (NB - 1) * LINKS

            def gates_of(it):
                m, one = (NB - 1) * IT + it, slice(it, it + 1)
                wait_sums(dve, NB - 1, it)
                nc.vector.scalar_tensor_tensor(out=z[:, it, :], in0=gcn[it][:, D:D + 2], scalar=unscale[:],
                                               in1=zc[:, m, :], op0=ALU.mult, op1=ALU.add).then_inc(z_set, 1)
                link(nc.vector.tensor_scalar(den[:, one], att[it][:, D:D + 1], q[:, m:m + 1], EPS_SUM, ALU.mult,
                                             ALU.add))
                link(nc.vector.reciprocal(rden[:, one], den[:, one]))
                dve.wait_ge(thz_done, NB + it)
                nc.vector.tensor_scalar(gate[:, it, :], th_z[:, it, :], 0.5, 0.5, ALU.mult,
                                        ALU.add).then_inc(gate_set, 1)
                dve.wait_ge(gate_set, NB + it)
                nc.vector.tensor_scalar(beta[:, one], gate[:, it, 1:2], unscale[:], None, ALU.mult)
                link(nc.vector.tensor_scalar(alpha2[:, one], rden[:, one], q_un[:, m:m + 1], gate[:, it, 0:1],
                                             ALU.mult, ALU.mult))

            def finish(it):
                m, one = (NB - 1) * IT + it, slice(it, it + 1)
                residual(NB - 1, it)
                dve.wait_ge(stats_done, m + 1)
                link(nc.vector.bn_aggr(mv[:, it, :], stats[:, it, :]))
                nc.vector.tensor_scalar(var_eps[:, one], mv[:, it, 1:2], EPS_VAR, None,
                                        ALU.add).then_inc(var_set, 1)
                dve.wait_ge(rstd_done, NB + it)
                nc.vector.tensor_scalar(x_r[:, m, :], res[:, it, :], mv[:, it, 0:1], rstd[:, one], ALU.subtract,
                                        ALU.mult).then_inc(res_out, 1)

            for it in range(IT):
                gates_of(it)
                mix(NB - 1, it, gcn[it][:, 0:D], att[it][:, 0:D])
                finish(it)

        @block.tensor
        def _(pe):
            pe.wait_ge(v_loaded, 16 * 3)
            for k in range(KT):
                for dk in range(KT):
                    ins = nc.tensor.matmul(gcn[0][:, 2 * k:2 * k + 2], wsat[:, dk, k * P:(k + 1) * P],
                                           acols[:, dk, :], start=(dk == 0), stop=(dk == KT - 1))
            ins.then_inc(v_done, 1)
            for c in range(NB):
                pe.wait_ge(x_loaded[c], 16)
                if c == 0:
                    pe.wait_ge(v_copied, 1)
                for t in range(c * IT, (c + 1) * IT):
                    for k in range(KT):
                        ins = nc.tensor.matmul(gcn[1][:, 6 * t:6 * t + 6], x_t[:, k, t * P:(t + 1) * P],
                                               w6[:, k, :], start=(k == 0), stop=(k == KT - 1))
                if c == NB - 1:
                    ins.then_inc(s6_done, 1)
                if c == 0:
                    pe.wait_ge(vl_set, KT)
                for k in range(KT):
                    ins = nc.tensor.matmul(att[c][:], vl_wide[:, k, :], x_t[:, k, c * IB:(c + 1) * IB],
                                           start=(k == 0), stop=(k == KT - 1))
                ins.then_inc(sl_done, 1)
            pe.wait_ge(w_split, KT)
            for t in range(JT):
                if t < IT:
                    pe.wait_ge(sl_copied, t + 1)
                else:
                    pe.wait_ge(rl_done, t - IT + 1)
                pe.wait_ge(xl_done, t // IT + 1)
                for k in range(KT):
                    xs = slice(k * N + t * P, k * N + (t + 1) * P)
                    for i, (xx, ww) in enumerate(((x_hi, w_hi), (x_hi, w_lo), (x_lo, w_hi))):
                        ins = nc.tensor.matmul(att[t % IT][:], xx[:, xs], ww[:, k, :],
                                               start=(k == 0 and i == 0), stop=(k == KT - 1 and i == 2))
                ins.then_inc(r_done, 1)
            pe.wait_ge(r_cols, 2)
            pe.wait_ge(s6_copied, 1)
            pe.wait_ge(rl_done, JT)
            pe.sem_inc(gcn_out, IT)
            pe.sem_inc(att_out, IT)

            last = NB - 1

            def adj_part(b, jt, it):
                a = adj[:, bass.ds((b * JT + jt) * IB + it * P, P)]
                if jt == 0:
                    pe.wait_ge(gcn_out, b * IT + it + 1)
                nc.tensor.matmul(gcn[it][:, 0:GC], a, r_hi[:, jt, G0:RC], start=(jt == 0), stop=False,
                                 skip_group_check=True)
                nc.tensor.matmul(gcn[it][:, 0:GC], a, r_lo[:, jt, G0:RC], start=False, stop=(jt == JT - 1),
                                 skip_group_check=True)

            def high_part(b, jt, it):
                f = f_hi[:, jt % ST, it * P:(it + 1) * P]
                if jt == 0:
                    pe.wait_ge(att_out, b * IT + it + 1)
                nc.tensor.matmul(att[it][:, 0:HC], f, r_hi[:, jt, 0:HC], start=(jt == 0), stop=False,
                                 skip_group_check=True)
                nc.tensor.matmul(att[it][:, 0:D], f, r_lo[:, jt, 0:D], start=False, stop=False,
                                 skip_group_check=True)

            def low_part(b, jt, it):
                ins = nc.tensor.matmul(att[it][:, 0:HC], f_lo[:, jt % ST, it * P:(it + 1) * P],
                                       r_hi[:, jt, 0:HC], start=False, stop=(jt == JT - 1),
                                       skip_group_check=True)
                if jt == JT - 1 and (it < IT - 1 or b is last):
                    ins.then_inc(sums_done, 1)
                return ins

            def unit(b, jt):
                n = b * JT + jt
                if jt % GJ == 0:
                    pe.wait_ge(adj_ready, b * NG + jt // GJ + 1)
                if jt in (0, JT - 1):
                    for it in range(IT):
                        adj_part(b, jt, it)
                        if it == 0:
                            pe.wait_ge(fh_done, n + 1)
                            pe.wait_ge(fl_done, n + 1)
                        high_part(b, jt, it)
                        ins = low_part(b, jt, it)
                else:
                    for it in range(IT):
                        adj_part(b, jt, it)
                    pe.wait_ge(fh_done, n + 1)
                    for it in range(IT):
                        high_part(b, jt, it)
                    pe.wait_ge(fl_done, n + 1)
                    for it in range(IT):
                        ins = low_part(b, jt, it)
                return ins

            with pe.Fori(0, NB - 1) as b:
                for jt in range(JT):
                    unit(b, jt).then_inc(unit_used, 1)
            for jt in range(JT - ST):
                unit(last, jt).then_inc(unit_used, 1)
            pe.wait_ge(adj_ready, NB * NG)
            for it in range(IT):
                for jt in range(JT - ST, JT):
                    adj_part(last, jt, it)
                    if it == 0:
                        pe.wait_ge(fh_done, last * JT + jt + 1)
                    high_part(last, jt, it)
                    if it == 0:
                        pe.wait_ge(fl_done, last * JT + jt + 1)
                    low_part(last, jt, it)


def kernel(x, adj, L0_gnn_W_sa, L0_gnn_a_sa, L0_gnn_W_gcnb, L0_gnn_b_gcnb, L0_gnn_Wa, L0_gnn_ba, L0_gnn_Wb,
           L0_gnn_bb):
    import numpy as np
    import concourse.bacc as bacc
    from concourse.bass_utils import run_bass_kernel_spmd

    x, adj = np.asarray(x), np.asarray(adj)
    w_sa, w_g = np.asarray(L0_gnn_W_sa), np.asarray(L0_gnn_W_gcnb)
    a_sa, wa, wb = np.asarray(L0_gnn_a_sa)[0], np.asarray(L0_gnn_Wa)[0], np.asarray(L0_gnn_Wb)[0]

    def rows(m):
        return np.ascontiguousarray(m.reshape(-1, P, m.shape[-1]).transpose(1, 0, 2))

    arrays = {
        "in_xT": rows(np.ascontiguousarray(x.T)),
        "in_xrows": rows(x),
        "in_adjT": np.ascontiguousarray(
            adj.T.reshape(JT, P, NB, IB).transpose(1, 2, 0, 3).reshape(P, NB * JT * IB)),
        "in_w": rows(np.concatenate([w_sa, w_g], axis=1)),
        "in_w_small": rows(np.stack([wa[:D], wb[:D], wa[D:], wb[D:]], axis=1)),
        "in_w_saT": rows(np.ascontiguousarray(w_sa.T)),
        "in_a_cols": rows(np.stack([a_sa[:D], a_sa[D:]], axis=1)),
        "in_b_row": np.ascontiguousarray(np.asarray(L0_gnn_b_gcnb)),
        "in_gate_bias": np.concatenate([np.asarray(L0_gnn_ba), np.asarray(L0_gnn_bb)]),
        "in_exponent": np.full((IT,), -0.5, np.float32),
    }
    nc = bacc.Bacc("TRN2", target_bir_lowering=False, num_devices=1)
    args = [nc.dram_tensor(name, a.shape, mybir.dt.from_np(a.dtype), kind="ExternalInput").ap()
            for name, a in arrays.items()]
    out = nc.dram_tensor("out_dram", (P, JT, D), F32, kind="ExternalOutput").ap()
    graph_layer(nc, *args, out)
    r = run_bass_kernel_spmd(nc, [arrays], core_ids=[0])
    got = r.results[0]["out_dram"]
    return np.ascontiguousarray(got.transpose(1, 0, 2).reshape(N, D))
```

```python
from contextlib import ExitStack
import math

import concourse.bass as bass
from concourse import mybir

F32 = mybir.dt.float32
F16 = mybir.dt.float16
BF16 = mybir.dt.bfloat16
ALU = mybir.AluOpType
ACT = mybir.ActivationFunctionType
AX = mybir.AxisListType
MAXABS = bass.bass_isa.ReduceOp.absmax
MAX = bass.bass_isa.ReduceOp.max

P = 128
N = 2048
D = 256
KT = D // P
JT = N // P
IB = 512
NB = N // IB
IT = IB // P
GJ = 4
NG = JT // GJ
RC = 2 * D + 4
HC = D + 1
G0 = D + 2
GC = D + 2
ST = 8
SF = 8
LEAK = 0.01
EPS_SUM = 1e-5
EPS_VAR = 1e-5
S6_AFTER = 3
RELU_AT = (5, 8)
EXP_AT = (7, 10)
CAST_AT = (8, 11)
LOW_AT = (10, 13)
PRE = len(RELU_AT)
TAIL = 7
GCN_BESIDE = {0: 2, 2: 3}
FSHIFT = 14 * math.log(2.0)
XTOP = 2.0 ** 14
RDOWN = 2.0 ** -21
BIG = 1e30
TINY = 1e-30
UNSCALE = 1.0 / (XTOP * XTOP * RDOWN)


def graph_layer(nc, xT, xrows, adjT, w_rhs, w_small, w_saT, a_cols, b_row, gate_bias, expo, out):
    with ExitStack() as ctx:
        def sb(name, shape, dt):
            return ctx.enter_context(nc.sbuf_tensor(name, shape, dt))

        def psum(name):
            return ctx.enter_context(nc.psum_tensor(name, [P, 512], F32))

        def sem(name):
            return ctx.enter_context(nc.semaphore(name))

        x_t = sb("x_t", [P, KT, N], F32)
        x_parts = sb("x_parts", [P, 2, KT * N], F16)
        x_hi, x_lo = x_parts[:, 0, :], x_parts[:, 1, :]
        w_f = sb("w_f", [P, KT, 2 * D], F32)
        w_hi = sb("w_hi", [P, KT, 2 * D], F16)
        w_lo = sb("w_lo", [P, KT, 2 * D], F16)
        w6 = sb("w6", [P, KT, 6], F32)
        wsat = sb("wsat", [P, KT, D], F32)
        acols = sb("acols", [P, KT, 2], F32)
        ones = sb("ones", [P, P], F32)
        vl_wide = sb("vl_wide", [P, KT, P], F32)
        peaks_x = sb("peaks_x", [P, NB], F32)
        peak_x = sb("peak_x", [P, 2], F32)
        peaks_w = sb("peaks_w", [P, 2], F32)
        peak_w = sb("peak_w", [P, 2], F32)
        top_x = sb("top_x", [P, 2], F32)
        top_w = sb("top_w", [P, 2], F32)
        inv_x = sb("inv_x", [P, 2], F32)
        inv_w = sb("inv_w", [P, 2], F32)
        scale_x = sb("scale_x", [P, 2], F32)
        r_first = sb("r_first", [P, 1], F32)
        scale_w = sb("scale_w", [P, 2], F32)
        w6_parts = sb("w6_parts", [P, KT, 12], F16)
        w6_hi, w6_lo = w6_parts[:, :, 0:6], w6_parts[:, :, 6:12]
        unscale6 = sb("unscale6", [P, 2], F32)
        unscale = sb("unscale", [P, 1], F32)
        rscale = sb("rscale", [P, 1], F32)
        s6_low = sb("s6_low", [P, JT, 6], F32)
        s6 = sb("s6", [P, JT, 6], F32)
        nsr = sb("nsr", [P, JT], F32)
        nsr_top = sb("nsr_top", [P, 1], F32)
        shift = sb("shift", [P, 1], F32)
        expo_f = sb("expo_f", [P, JT], F32)
        expo_q = sb("expo_q", [P, 1], F32)
        q = sb("q", [P, JT], F32)
        q_un = sb("q_un", [P, JT], F32)
        zc = sb("zc", [P, JT, 2], F32)
        zbias = sb("zbias", [P, 2], F32)
        bg = sb("bg", [P, D], F32)
        halfpow = sb("halfpow", [P, IT], F32)
        u_f = sb("u_f", [P, JT, 2], F32)
        sl_wide = sb("sl_wide", [P, N], F32)
        adj = sb("adj", [P, NB * JT * IB], F16)
        miss = sb("miss", [P, 2, GJ * IB], BF16)
        f_32 = sb("f_32", [P, SF, IB], F32)
        f_hi = sb("f_hi", [P, ST, IB], F16)
        f_lo = sb("f_lo", [P, ST, IB], F16)
        r_hi = sb("r_hi", [P, JT, RC], F16)
        r_lo = sb("r_lo", [P, JT, RC], F16)
        x_r = sb("x_r", [P, JT, D], F32)
        mix_a, mix_b, mix_c, th = (x_t[:, k, h * IT * D:(h + 1) * IT * D].rearrange("p (t d) -> p t d", t=IT)
                                   for k in range(KT) for h in range(2))
        late = x_parts[:].rearrange("p a b -> p (a b)").bitcast(F32)
        res = late[:, 0:IT * D].rearrange("p (t d) -> p t d", t=IT)
        att_s = late[:, IT * D:IT * (D + GC)].rearrange("p (t d) -> p t d", t=IT)
        gcn_s = late[:, IT * (D + GC):IT * (D + 2 * GC)].rearrange("p (t d) -> p t d", t=IT)
        z = sb("z", [P, IT, 2], F32)
        th_z = sb("th_z", [P, IT, 2], F32)
        gate = sb("gate", [P, IT, 2], F32)
        den = sb("den", [P, IT], F32)
        rden = sb("rden", [P, IT], F32)
        alpha = sb("alpha", [P, IT], F32)
        alpha2 = sb("alpha2", [P, IT], F32)
        stats = sb("stats", [P, IT, 6], F32)
        mean2 = sb("mean2", [P, IT], F32)
        spread = sb("spread", [P, IT], F32)
        diff = sb("diff", [P, IT], F32)
        diff2 = sb("diff2", [P, IT], F32)
        mean = sb("mean", [P, IT], F32)
        var_in = sb("var_in", [P, IT], F32)
        mv = sb("mv", [P, IT, 2], F32)
        var_eps = sb("var_eps", [P, IT], F32)
        rstd = sb("rstd", [P, IT], F32)
        nmr = sb("nmr", [P, IT], F32)

        att = [psum(f"att{i}") for i in range(IT)]
        gcn = [psum(f"gcn{i}") for i in range(IT)]

        v_loaded = sem("v_loaded")
        w_loaded = sem("w_loaded")
        misc_loaded = sem("misc_loaded")
        x_loaded = [sem(f"x_loaded{c}") for c in range(NB)]
        peak_parts = sem("peak_parts")
        rows_loaded = sem("rows_loaded")
        adj_dma = [sem(f"adj_dma{i}") for i in range(4)]
        adj_ready = sem("adj_ready")
        ones_set = sem("ones_set")
        v_done = sem("v_done")
        v_copied = sem("v_copied")
        vl_set = sem("vl_set")
        s6_done = sem("s6_done")
        s6_copied = sem("s6_copied")
        sl_done = sem("sl_done")
        sl_copied = sem("sl_copied")
        peak_w_done = sem("peak_w_done")
        peak_x_done = sem("peak_x_done")
        top_w_done = sem("top_w_done")
        top_x_done = sem("top_x_done")
        dve_step = sem("dve_step")
        scale_w_set = sem("scale_w_set")
        scale_x_set = sem("scale_x_set")
        r_first_set = sem("r_first_set")
        w6_split = sem("w6_split")
        nsr_top_done = sem("nsr_top_done")
        shift_done = sem("shift_done")
        expo_set = sem("expo_set")
        q_done = sem("q_done")
        wh_done = sem("wh_done")
        w_split = sem("w_split")
        xh_done = sem("xh_done")
        xl_done = sem("xl_done")
        r_done = sem("r_done")
        rh_done = sem("rh_done")
        rl_done = sem("rl_done")
        r_cols = sem("r_cols")
        miss_set = sem("miss_set")
        relu_done = sem("relu_done")
        f32_done = sem("f32_done")
        fh_done = sem("fh_done")
        fl_done = sem("fl_done")
        gcn_sums = sem("gcn_sums")
        sums_done = sem("sums_done")
        unit_used = sem("unit_used")
        att_out = sem("att_out")
        gcn_out = sem("gcn_out")
        z_set = sem("z_set")
        thz_done = sem("thz_done")
        gate_set = sem("gate_set")
        mixa_done = sem("mixa_done")
        mixc_done = sem("mixc_done")
        th_done = sem("th_done")
        var_set = sem("var_set")
        rstd_done = sem("rstd_done")
        norm_set = sem("norm_set")
        half_added = sem("half_added")
        mixb_done = sem("mixb_done")
        res_done = sem("res_done")
        stats_done = sem("stats_done")
        res_out = sem("res_out")
        last_out = sem("last_out")
        stored = sem("stored")

        block = ctx.enter_context(nc.Block())

        x_hi3 = x_hi.rearrange("p (k i) -> p k i", k=KT)
        x_lo3 = x_lo.rearrange("p (k i) -> p k i", k=KT)

        r_banks = [*att, *gcn[2:]]

        def chunk_scale(c):
            return scale_x[:, min(c, 1):min(c, 1) + 1]

        def down(t):
            return r_first[:] if t < IT else RDOWN

        def r_bank(t):
            return r_banks[t % len(r_banks)][:].rearrange("p (h d) -> p h d", h=2)

        def halves(r, t):
            return r[:, t, 0:2 * G0].rearrange("p (h d) -> p h d", h=2)[:, :, 0:D]

        def wait_sums(eng, b, it):
            if it == IT - 1 and not (isinstance(b, int) and b == NB - 1):
                eng.wait_ge(unit_used, b * JT + JT)
            else:
                eng.wait_ge(sums_done, b * (IT - 1) + it + 1)

        @block.sync
        def _(sp):
            sp.dma_start(wsat[:], w_saT).then_inc(v_loaded, 16)
            sp.dma_start(acols[:], a_cols).then_inc(v_loaded, 16)
            sp.dma_start(w6[:, :, 0:4], w_small).then_inc(v_loaded, 16)
            for c in range(NB):
                if c == NB - 1:
                    sp.dma_start(w_f[:], w_rhs).then_inc(w_loaded, 16)
                sp.dma_start(x_t[:, :, c * IB:(c + 1) * IB], xT[:, :, c * IB:(c + 1) * IB]).then_inc(x_loaded[c], 16)
            sp.dma_start(zbias[:], gate_bias.partition_broadcast(P)).then_inc(misc_loaded, 16)
            sp.dma_start(bg[:], b_row.partition_broadcast(P)).then_inc(misc_loaded, 16)
            sp.dma_start(halfpow[:], expo.partition_broadcast(P)).then_inc(misc_loaded, 16)
            sp.wait_ge(adj_ready, NG)
            sp.dma_start(x_r[:], xrows).then_inc(rows_loaded, 16)
            with sp.Fori(0, NB - 1) as b:
                sp.wait_ge(res_out, b * IT + IT)
                sp.dma_start(out[:, bass.ds(b * IT, IT), :],
                             x_r[:, bass.ds(b * IT, IT), :]).then_inc(stored, 16)
            for m in range(JT - IT, JT):
                if m < JT - 1:
                    sp.wait_ge(res_out, m + 1)
                else:
                    sp.wait_ge(last_out, 1)
                sp.dma_start(out[:, m, :], x_r[:, m, :]).then_inc(stored, 16)
            sp.wait_ge(stored, (NB - 1 + IT) * 16)

        @block.gpsimd
        def _(pool):
            def load_adj(n):
                pool.dma_start(adj[:, n * GJ * IB:(n + 1) * GJ * IB],
                               adjT[:, n * GJ * IB:(n + 1) * GJ * IB]).then_inc(adj_dma[n % 4], 16)

            def landed(n):
                pool.wait_ge(adj_dma[n % 4], 16 * (n // 4 + 1))
                pool.sem_inc(adj_ready, 1)

            def top_of_x(g):
                pool.wait_ge(peak_x_done, g + 1)
                nc.gpsimd.partition_all_reduce(top_x[:, g:g + 1], peak_x[:, g:g + 1], P,
                                               MAXABS).then_inc(top_x_done, 1)

            top_of_x(0)
            pool.wait_ge(peak_w_done, 1)
            nc.gpsimd.partition_all_reduce(top_w[:], peak_w[:], P, MAXABS).then_inc(top_w_done, 1)
            top_of_x(1)
            load_adj(0)
            load_adj(1)
            landed(0)
            pool.wait_ge(nsr_top_done, 1)
            nc.gpsimd.partition_all_reduce(shift[:], nsr_top[:], P, MAX).then_inc(shift_done, 1)
            load_adj(2)
            load_adj(3)
            for n in range(4, NB * NG):
                load_adj(n)
                landed(n - 3)
            for n in range(NB * NG - 3, NB * NG):
                landed(n)
            pool.wait_ge(misc_loaded, 16 * 3)
            with pool.Fori(0, NB - 1) as b:
                pool.wait_ge(var_set, b + 1)
                nc.gpsimd.tensor_tensor(rstd[:], var_eps[:], halfpow[:], ALU.pow).then_inc(rstd_done, 1)
            for it in range(IT):
                pool.wait_ge(var_set, NB + it)
                nc.gpsimd.tensor_tensor(rstd[:, it:it + 1], var_eps[:, it:it + 1], halfpow[:, it:it + 1],
                                        ALU.pow).then_inc(rstd_done, 1)

        @block.scalar
        def _(act):
            def exp_f(p, h, jt):
                act.wait_ge(relu_done, 2 * p + h + 1)
                nc.scalar.activation(f_32[:, jt % SF, :], f_32[:, jt % SF, :], ACT.Exp,
                                     bias=expo_f[:, jt:jt + 1], scale=-(1.0 - LEAK)).then_inc(f32_done, 1)

            def cast_f(p, jt):
                act.wait_ge(f32_done, 2 * p + 2)
                if not isinstance(p, int) or 2 * p >= ST:
                    act.wait_ge(unit_used, 2 * p - ST + 2)
                nc.scalar.copy(f_hi[:, jt % ST:jt % ST + 2, :], f_32[:, jt % SF:jt % SF + 2, :])\
                  .then_inc(fh_done, 1)

            def pair(p, jt):
                exp_f(p, 0, jt)
                exp_f(p, 1, jt + 1)
                if not isinstance(p, int) or p > PRE:
                    cast_f(p - 1, (jt - 2) % JT)

            def sl_copy(c):
                act.wait_ge(sl_done, c + 1)
                nc.scalar.copy(sl_wide[:, c * IB:(c + 1) * IB], att[c][:]).then_inc(sl_copied, 1)

            def x_high(c):
                act.wait_ge(scale_x_set, min(c, 1) + 1)
                nc.scalar.activation(x_hi3[:, :, c * IB:(c + 1) * IB], x_t[:, :, c * IB:(c + 1) * IB], ACT.Copy,
                                     scale=chunk_scale(c)).then_inc(xh_done, 1)

            act.wait_ge(v_done, 1)
            nc.scalar.copy(w6[:, :, 4:6], gcn[0][:, 0:2 * KT].rearrange("p (k c) -> p k c", k=KT))\
              .then_inc(v_copied, 1)
            act.wait_ge(ones_set, 1)
            act.wait_ge(v_copied, 1)
            for k in range(KT):
                nc.scalar.activation(vl_wide[:, k, :], ones[:], ACT.Copy, scale=w6[:, k, 4:5]).then_inc(vl_set, 1)
            x_high(0)
            sl_copy(0)
            act.wait_ge(scale_w_set, 1)
            for k in range(KT):
                nc.scalar.activation(w_hi[:, k, :], w_f[:, k, :], ACT.Copy,
                                     scale=scale_w[:, 0:1]).then_inc(wh_done, 1)
            sl_copy(1)
            x_high(1)
            x_high(2)
            sl_copy(2)
            x_high(3)
            sl_copy(3)
            act.wait_ge(r_first_set, 1)
            for t in range(JT):
                act.wait_ge(r_done, t + 1)
                nc.scalar.activation(halves(r_hi, t), r_bank(t), ACT.Copy, scale=down(t)).then_inc(rh_done, 1)
                if t == S6_AFTER + 2:
                    act.wait_ge(expo_set, 1)
                    nc.scalar.activation(q[:], s6[:, :, 4], ACT.Exp, bias=expo_q[:], scale=-LEAK).then_inc(q_done, 1)
                if t in EXP_AT:
                    exp_f(EXP_AT.index(t), 0, 2 * EXP_AT.index(t))
                    exp_f(EXP_AT.index(t), 1, 2 * EXP_AT.index(t) + 1)
                if t in CAST_AT:
                    cast_f(CAST_AT.index(t), 2 * CAST_AT.index(t))
            for p in range(PRE, JT // 2):
                pair(p, 2 * p)
                if p < IT + PRE:
                    g = p - PRE
                    act.wait_ge(rows_loaded, 16)
                    nc.scalar.activation(x_r[:, g * IT:(g + 1) * IT, :], x_r[:, g * IT:(g + 1) * IT, :],
                                         ACT.Copy, bias=0.5).then_inc(half_added, 1)

            def sums_copy(b):
                for it in range(IT):
                    wait_sums(act, b, it)
                    nc.scalar.copy(gcn_s[:, it, :], gcn[it][:, 0:GC]).then_inc(gcn_out, 1)
                    nc.scalar.copy(att_s[:, it, 0:HC], att[it][:, 0:HC]).then_inc(att_out, 1)

            def normalise(b):
                act.wait_ge(norm_set, b + 1)
                for it in range(IT):
                    nc.scalar.activation(x_r[:, bass.ds(b * IT + it, 1), :], res[:, it, :], ACT.Identity,
                                         scale=rstd[:, it:it + 1], bias=nmr[:, it:it + 1]).then_inc(res_out, 1)

            def tanh_gates(b):
                act.wait_ge(z_set, b + 1)
                nc.scalar.activation(th_z[:], z[:], ACT.Tanh, scale=0.5).then_inc(thz_done, 1)

            def gated_gcn(b, it, gates):
                act.wait_ge(mixa_done, b * IT + it + 1)
                act.wait_ge(gate_set, gates)
                nc.scalar.activation(mix_b[:, it, :], mix_a[:, it, :], ACT.Copy,
                                     scale=gate[:, it, 1:2]).then_inc(mixb_done, 1)

            def tanh_mix(b, it):
                act.wait_ge(mixc_done, b * IT + it + 1)
                nc.scalar.activation(th[:, it, :], mix_c[:, it, :], ACT.Tanh, scale=0.5).then_inc(th_done, 1)

            act.wait_ge(misc_loaded, 16 * 3)

            def block_steps(b):
                for h in range(JT // 2):
                    pair(b * (JT // 2) + h, 2 * h)
                    if h == 2:
                        sums_copy(b - 1)
                    if h == 3:
                        tanh_gates(b - 1)
                    if h == 4:
                        for it in range(IT):
                            gated_gcn(b - 1, it, b)
                    if h == 5:
                        for it in range(IT):
                            tanh_mix(b - 1, it)

            with act.Fori(1, NB - 1) as b:
                block_steps(b)
                normalise(b - 1)
            block_steps(NB - 1)
            cast_f(NB * JT // 2 - 1, JT - 2)
            normalise(NB - 2)

            def gate_tanh(it):
                act.wait_ge(z_set, NB + it)
                nc.scalar.activation(th_z[:, it, :], z[:, it, :], ACT.Tanh, scale=0.5).then_inc(thz_done, 1)

            def tile_normalise(it):
                act.wait_ge(norm_set, NB + it)
                nc.scalar.activation(x_r[:, (NB - 1) * IT + it, :], res[:, it, :], ACT.Identity,
                                     scale=rstd[:, it:it + 1], bias=nmr[:, it:it + 1]).then_inc(res_out, 1)

            gate_tanh(0)
            gate_tanh(1)
            gated_gcn(NB - 1, 0, NB)
            for it in range(IT):
                if it == IT - 1:
                    gated_gcn(NB - 1, it, NB + it)
                if it + 1 < IT - 1:
                    gated_gcn(NB - 1, it + 1, NB + it + 1)
                tanh_mix(NB - 1, it)
                if it in GCN_BESIDE:
                    gate_tanh(GCN_BESIDE[it])
                if it >= 1:
                    tile_normalise(it - 1)

        @block.vector
        def _(dve):
            chain = [0]

            def link(ins):
                chain[0] += 1
                ins.then_inc(dve_step, 1)
                dve.wait_ge(dve_step, chain[0])

            def missing(b, g):
                dve.wait_ge(adj_ready, b * NG + g + 1)
                nc.vector.tensor_scalar(miss[:, g % 2, :], adj[:, bass.ds((b * NG + g) * GJ * IB, GJ * IB)],
                                        0.0, BIG, ALU.is_equal, ALU.mult).then_inc(miss_set, 1)

            def masked_relu(b, jt):
                dve.wait_ge(miss_set, b * NG + jt // GJ + 1)
                nc.vector.scalar_tensor_tensor(
                    out=f_32[:, jt % SF, :], in0=sl_wide[:, bass.ds(b * IB, IB)], scalar=s6[:, jt, 5:6],
                    in1=miss[:, (jt // GJ) % 2, (jt % GJ) * IB:(jt % GJ + 1) * IB],
                    op0=ALU.add, op1=ALU.max).then_inc(relu_done, 1)

            def low_part(p, jt):
                dve.wait_ge(fh_done, p + 1)
                if not isinstance(p, int) or 2 * p >= ST:
                    dve.wait_ge(unit_used, 2 * p - ST + 2)
                nc.vector.tensor_tensor(f_lo[:, jt % ST:jt % ST + 2, :], f_32[:, jt % SF:jt % SF + 2, :],
                                        f_hi[:, jt % ST:jt % ST + 2, :], ALU.subtract).then_inc(fl_done, 1)

            def relus(b, jt):
                if jt % GJ == 0:
                    missing(b, jt // GJ)
                masked_relu(b, jt)
                masked_relu(b, jt + 1)

            def pair(p, b, jt):
                relus(b, jt)
                if not isinstance(p, int) or p >= PRE + 2:
                    low_part(p - 2, (jt - 4) % JT)

            def x_low(c):
                dve.wait_ge(xh_done, c + 1)
                nc.vector.scalar_tensor_tensor(
                    out=x_lo3[:, :, c * IB:(c + 1) * IB], in0=x_t[:, :, c * IB:(c + 1) * IB],
                    scalar=chunk_scale(c), in1=x_hi3[:, :, c * IB:(c + 1) * IB],
                    op0=ALU.mult, op1=ALU.subtract).then_inc(xl_done, 1)

            nc.vector.memset(ones[:], 1.0).then_inc(ones_set, 1)
            nc.vector.memset(r_hi[:, :, D:D + 2], 1.0).then_inc(r_cols, 1)

            def peak_of_x(c):
                dve.wait_ge(x_loaded[c], 16)
                nc.vector.tensor_reduce(peaks_x[:, c:c + 1], x_t[:, :, c * IB:(c + 1) * IB], AX.XY, ALU.max,
                                        apply_absolute_value=True).then_inc(peak_parts, 1)

            def scale_of_x(g):
                dve.wait_ge(top_x_done, g + 1)
                link(nc.vector.reciprocal(inv_x[:, g:g + 1], top_x[:, g:g + 1]))
                nc.vector.tensor_scalar(scale_x[:, g:g + 1], inv_x[:, g:g + 1], XTOP, None,
                                        ALU.mult).then_inc(scale_x_set, 1)

            peak_of_x(0)
            dve.wait_ge(peak_parts, 1)
            nc.vector.tensor_scalar(peak_x[:, 0:1], peaks_x[:, 0:1], TINY, None, ALU.max).then_inc(peak_x_done, 1)
            dve.wait_ge(v_copied, 1)
            nc.vector.tensor_reduce(peaks_w[:, 1:2], w6[:], AX.XY, ALU.max, apply_absolute_value=True)
            peak_of_x(1)
            scale_of_x(0)
            peak_of_x(2)
            dve.wait_ge(w_loaded, 16)
            link(nc.vector.tensor_reduce(peaks_w[:, 0:1], w_f[:], AX.XY, ALU.max, apply_absolute_value=True))
            nc.vector.tensor_tensor(peak_w[:, 0:1], peaks_w[:, 0:1], peaks_w[:, 1:2], ALU.max)
            nc.vector.tensor_scalar(peak_w[:, 1:2], peaks_w[:, 1:2], TINY, None, ALU.max).then_inc(peak_w_done, 1)
            peak_of_x(3)
            dve.wait_ge(peak_parts, NB)
            link(nc.vector.tensor_reduce(peaks_x[:, 0:1], peaks_x[:], AX.X, ALU.max))
            nc.vector.tensor_scalar(peak_x[:, 1:2], peaks_x[:, 0:1], TINY, None, ALU.max).then_inc(peak_x_done, 1)
            dve.wait_ge(top_w_done, 1)
            link(nc.vector.tensor_scalar(top_w[:, 0:1], top_w[:, 0:1], TINY, None, ALU.max))
            link(nc.vector.reciprocal(inv_w[:], top_w[:]))
            nc.vector.tensor_scalar(scale_w[:], inv_w[:], XTOP, None, ALU.mult).then_inc(scale_w_set, 1)
            x_low(0)
            scale_of_x(1)
            nc.vector.tensor_scalar(r_first[:], top_x[:, 0:1], inv_x[:, 1:2], RDOWN, ALU.mult,
                                    ALU.mult).then_inc(r_first_set, 1)
            for k in range(KT):
                dve.wait_ge(wh_done, k + 1)
                nc.vector.scalar_tensor_tensor(out=w_lo[:, k, :], in0=w_f[:, k, :], scalar=scale_w[:, 0:1],
                                               in1=w_hi[:, k, :], op0=ALU.mult,
                                               op1=ALU.subtract).then_inc(w_split, 1)
            dve.wait_ge(scale_w_set, 1)
            link(nc.vector.tensor_scalar(w6_hi, w6[:], scale_w[:, 1:2], None, ALU.mult))
            nc.vector.scalar_tensor_tensor(out=w6_lo, in0=w6[:], scalar=scale_w[:, 1:2], in1=w6_hi,
                                           op0=ALU.mult, op1=ALU.subtract).then_inc(w6_split, 1)
            nc.vector.tensor_scalar(unscale[:], top_x[:, 1:2], top_w[:, 0:1], UNSCALE, ALU.mult, ALU.mult)
            nc.vector.tensor_scalar(unscale6[:], top_x[:], top_w[:, 1:2], 1.0 / (XTOP * XTOP), ALU.mult, ALU.mult)
            dve.wait_ge(scale_x_set, 2)
            link(nc.vector.tensor_scalar(rscale[:], scale_x[:, 1:2], scale_w[:, 0:1], RDOWN, ALU.mult, ALU.mult))
            for c in range(1, NB):
                x_low(c)

            def small_columns():
                dve.wait_ge(s6_done, 1)
                products = gcn[1][:, 0:JT * 12].rearrange("p (t c) -> p t c", t=JT)
                link(nc.vector.tensor_copy(s6_low[:], products[:, :, 6:12]))
                link(nc.vector.tensor_tensor(s6[:], products[:, :, 0:6], s6_low[:], ALU.add))
                for g, tiles in enumerate((slice(0, IT), slice(IT, JT))):
                    nc.vector.tensor_scalar(s6[:, tiles, :], s6[:, tiles, :], unscale6[:, g:g + 1], None,
                                            ALU.mult).then_inc(s6_copied, 1)
                dve.wait_ge(s6_copied, 2)
                link(nc.vector.tensor_scalar(nsr[:], s6[:, :, 5], -LEAK, None, ALU.mult))
                nc.vector.tensor_reduce(nsr_top[:], nsr[:], AX.X, ALU.max).then_inc(nsr_top_done, 1)
                link(nc.vector.tensor_scalar(u_f[:], s6[:, :, 0:2], rscale[:], None, ALU.mult))
                link(nc.vector.tensor_copy(r_hi[:, :, G0 + D:G0 + D + 2], u_f[:]))
                nc.vector.tensor_tensor(r_lo[:, :, G0 + D:G0 + D + 2], u_f[:], r_hi[:, :, G0 + D:G0 + D + 2],
                                        ALU.subtract).then_inc(r_cols, 1)
                dve.wait_ge(misc_loaded, 16 * 3)
                for c in range(2):
                    nc.vector.tensor_scalar(zc[:, :, c], s6[:, :, 2 + c], zbias[:, c:c + 1], None, ALU.add)

            def exponents():
                dve.wait_ge(shift_done, 1)
                nc.vector.tensor_scalar(expo_q[:], shift[:], -FSHIFT, None, ALU.add)
                nc.vector.tensor_scalar(expo_f[:], nsr[:], shift[:], FSHIFT, ALU.subtract, ALU.add)\
                  .then_inc(expo_set, 1)

            dve.wait_ge(sl_copied, 1)
            for t in range(JT):
                dve.wait_ge(rh_done, t + 1)
                nc.vector.scalar_tensor_tensor(
                    out=halves(r_lo, t), in0=r_bank(t), scalar=down(t),
                    in1=halves(r_hi, t), op0=ALU.mult, op1=ALU.subtract).then_inc(rl_done, 1)
                if t == S6_AFTER:
                    small_columns()
                if t == S6_AFTER + 1:
                    exponents()
                if t in RELU_AT:
                    relus(0, 2 * RELU_AT.index(t))
                if t in LOW_AT:
                    low_part(LOW_AT.index(t), 2 * LOW_AT.index(t))
            dve.wait_ge(q_done, 1)
            nc.vector.tensor_scalar(q_un[:], q[:], unscale[:], None, ALU.mult)
            for p in range(PRE, JT // 2):
                pair(p, 0, 2 * p)

            base = chain[0]
            LINKS = 7

            def block_link(b, k, ins):
                ins.then_inc(dve_step, 1)
                dve.wait_ge(dve_step, base + b * LINKS + k + 1)

            def gates_in(b):
                dve.wait_ge(gcn_out, (b + 1) * IT + IT)
                nc.vector.scalar_tensor_tensor(out=z[:], in0=gcn_s[:, :, D:D + 2], scalar=unscale[:],
                                               in1=zc[:, bass.ds(b * IT, IT), :], op0=ALU.mult,
                                               op1=ALU.add).then_inc(z_set, 1)
                dve.wait_ge(att_out, (b + 1) * IT + IT)
                block_link(b, 0, nc.vector.tensor_tensor(den[:], att_s[:, :, D], q[:, bass.ds(b * IT, IT)],
                                                         ALU.mult))
                block_link(b, 1, nc.vector.tensor_scalar(den[:], den[:], EPS_SUM, None, ALU.add))
                block_link(b, 2, nc.vector.reciprocal(rden[:], den[:]))
                block_link(b, 3, nc.vector.tensor_tensor(alpha[:], rden[:], q_un[:, bass.ds(b * IT, IT)],
                                                         ALU.mult))

            def gates_out(b):
                dve.wait_ge(thz_done, b + 1)
                nc.vector.tensor_scalar(gate[:], th_z[:], 0.5, 0.5, ALU.mult, ALU.add).then_inc(gate_set, 1)
                dve.wait_ge(gate_set, b + 1)
                block_link(b, 4, nc.vector.tensor_tensor(alpha2[:], alpha[:], gate[:, :, 0], ALU.mult))

            def gcn_message(it, gcn_in):
                nc.vector.scalar_tensor_tensor(out=mix_a[:, it, :], in0=gcn_in, scalar=unscale[:], in1=bg[:],
                                               op0=ALU.mult, op1=ALU.add).then_inc(mixa_done, 1)

            def mix_att(b, it, att_in):
                dve.wait_ge(mixb_done, b * IT + it + 1)
                nc.vector.scalar_tensor_tensor(out=mix_c[:, it, :], in0=att_in, scalar=alpha2[:, it:it + 1],
                                               in1=mix_b[:, it, :], op0=ALU.mult,
                                               op1=ALU.add).then_inc(mixc_done, 1)

            def residual(b, it):
                dve.wait_ge(th_done, b * IT + it + 1)
                nc.vector.scalar_tensor_tensor(out=res[:, it, :], in0=th[:, it, :], scalar=0.5,
                                               in1=x_r[:, bass.ds(b * IT + it, 1), :], op0=ALU.mult,
                                               op1=ALU.add).then_inc(res_done, 1)
                dve.wait_ge(res_done, b * IT + it + 1)
                nc.vector.bn_stats(stats[:, it, :], res[:, it, :]).then_inc(stats_done, 1)

            def variance(b):
                dve.wait_ge(stats_done, b * IT + IT)
                nc.vector.tensor_tensor(mean2[:], stats[:, :, 1], stats[:, :, 4], ALU.add)
                nc.vector.tensor_tensor(spread[:], stats[:, :, 2], stats[:, :, 5], ALU.add)
                block_link(b, 5, nc.vector.tensor_tensor(diff[:], stats[:, :, 1], stats[:, :, 4], ALU.subtract))
                nc.vector.tensor_scalar(mean[:], mean2[:], 0.5, None, ALU.mult)
                nc.vector.tensor_scalar(var_in[:], spread[:], 1.0 / D, EPS_VAR, ALU.mult, ALU.add)
                block_link(b, 6, nc.vector.tensor_tensor(diff2[:], diff[:], diff[:], ALU.mult))
                nc.vector.scalar_tensor_tensor(out=var_eps[:], in0=diff2[:], scalar=0.25, in1=var_in[:],
                                               op0=ALU.mult, op1=ALU.add).then_inc(var_set, 1)

            def norm_bias(b):
                dve.wait_ge(rstd_done, b + 1)
                nc.vector.scalar_tensor_tensor(out=nmr[:], in0=mean[:], scalar=-1.0, in1=rstd[:], op0=ALU.mult,
                                               op1=ALU.mult).then_inc(norm_set, 1)

            dve.wait_ge(half_added, IT)
            dve.wait_ge(sl_copied, NB)

            def block_steps(b):
                for h in range(JT // 2):
                    pair(b * (JT // 2) + h, b, 2 * h)
                    if h == 3:
                        gates_in(b - 1)
                        for it in range(IT):
                            gcn_message(it, gcn_s[:, it, 0:D])
                    if h == 4:
                        gates_out(b - 1)
                    if h == 5:
                        for it in range(IT):
                            mix_att(b - 1, it, att_s[:, it, 0:D])
                    if h == 6:
                        for it in range(IT):
                            residual(b - 1, it)
                        variance(b - 1)

            with dve.Fori(1, NB - 1) as b:
                block_steps(b)
                norm_bias(b - 1)
            block_steps(NB - 1)
            norm_bias(NB - 2)
            low_part(NB * JT // 2 - 2, JT - 4)
            low_part(NB * JT // 2 - 1, JT - 2)

            chain[0] = base + (NB - 1) * LINKS

            def mark(ins):
                chain[0] += 1
                ins.then_inc(dve_step, 1)
                return chain[0]

            def gate_input(it):
                dve.wait_ge(gcn_sums, it + 1)
                nc.vector.scalar_tensor_tensor(out=z[:, it, :], in0=gcn[it][:, D:D + 2], scalar=unscale[:],
                                               in1=zc[:, (NB - 1) * IT + it, :], op0=ALU.mult,
                                               op1=ALU.add).then_inc(z_set, 1)

            def gcn_of(it):
                gate_input(it)
                gcn_message(it, gcn[it][:, 0:D])

            def gates_of(it):
                dve.wait_ge(thz_done, NB + it)
                nc.vector.tensor_scalar(gate[:, it, :], th_z[:, it, :], 0.5, 0.5, ALU.mult,
                                        ALU.add).then_inc(gate_set, 1)

            def tile_steps(it):
                m, one = (NB - 1) * IT + it, slice(it, it + 1)
                wait_sums(dve, NB - 1, it)
                den_set = mark(nc.vector.tensor_scalar(den[:, one], att[it][:, D:D + 1], q[:, m:m + 1], EPS_SUM,
                                                       ALU.mult, ALU.add))
                if it + 1 < IT - 1:
                    gates_of(it + 1)
                dve.wait_ge(dve_step, den_set)
                rden_set = mark(nc.vector.reciprocal(rden[:, one], den[:, one]))
                dve.wait_ge(dve_step, rden_set)
                alpha_set = mark(nc.vector.tensor_scalar(alpha2[:, one], rden[:, one], q_un[:, m:m + 1],
                                                         gate[:, it, 0:1], ALU.mult, ALU.mult))
                dve.wait_ge(dve_step, alpha_set)
                mix_att(NB - 1, it, att[it][:, 0:D])
                if it >= 1:
                    tile_norm_bias(it - 1)
                if it in GCN_BESIDE:
                    gcn_of(GCN_BESIDE[it])
                residual(NB - 1, it)
                dve.wait_ge(stats_done, m + 1)
                mv_set = mark(nc.vector.bn_aggr(mv[:, it, :], stats[:, it, :]))
                dve.wait_ge(dve_step, mv_set)
                nc.vector.tensor_scalar(var_eps[:, one], mv[:, it, 1:2], EPS_VAR, None,
                                        ALU.add).then_inc(var_set, 1)

            def tile_norm_bias(it):
                one = slice(it, it + 1)
                dve.wait_ge(rstd_done, NB + it)
                nc.vector.scalar_tensor_tensor(out=nmr[:, one], in0=mv[:, it, 0:1], scalar=-1.0,
                                               in1=rstd[:, one], op0=ALU.mult, op1=ALU.mult)\
                  .then_inc(norm_set, 1)

            def normalise_last():
                it = IT - 1
                dve.wait_ge(rstd_done, NB + it)
                nc.vector.tensor_scalar(x_r[:, JT - 1, :], res[:, it, :], mv[:, it, 0:1], rstd[:, it:it + 1],
                                        ALU.subtract, ALU.mult).then_inc(last_out, 1)

            gcn_of(0)
            gcn_of(1)
            gates_of(0)
            for it in range(IT):
                if it == IT - 1:
                    gates_of(it)
                tile_steps(it)
            normalise_last()

        @block.tensor
        def _(pe):
            pe.wait_ge(v_loaded, 16 * 3)
            for k in range(KT):
                for dk in range(KT):
                    ins = nc.tensor.matmul(gcn[0][:, 2 * k:2 * k + 2], wsat[:, dk, k * P:(k + 1) * P],
                                           acols[:, dk, :], start=(dk == 0), stop=(dk == KT - 1))
            ins.then_inc(v_done, 1)
            pe.wait_ge(vl_set, KT)
            for c in range(NB):
                pe.wait_ge(x_loaded[c], 16)
                for k in range(KT):
                    ins = nc.tensor.matmul(att[c][:], vl_wide[:, k, :], x_t[:, k, c * IB:(c + 1) * IB],
                                           start=(k == 0), stop=(k == KT - 1))
                ins.then_inc(sl_done, 1)

            def x_products(out_ap, t):
                for k in range(KT):
                    if t == 0:
                        pe.wait_ge(w_split, k + 1)
                    xs = slice(k * N + t * P, k * N + (t + 1) * P)
                    for i, (xx, ww) in enumerate(((x_hi, w_hi), (x_hi, w_lo), (x_lo, w_hi))):
                        ins = nc.tensor.matmul(out_ap, xx[:, xs], ww[:, k, :],
                                               start=(k == 0 and i == 0), stop=(k == KT - 1 and i == 2))
                return ins

            def small_products(m):
                for k in range(KT):
                    xs = slice(k * N + m * P, k * N + (m + 1) * P)
                    nc.tensor.matmul(gcn[1][:, 12 * m:12 * m + 12], x_hi[:, xs], w6_parts[:, k, :],
                                     start=(k == 0), stop=False, skip_group_check=True)
                    ins = nc.tensor.matmul(gcn[1][:, 12 * m:12 * m + 6], x_lo[:, xs], w6_parts[:, k, 0:6],
                                           start=False, stop=(k == KT - 1), skip_group_check=True)
                return ins

            for t in range(JT):
                if t >= len(r_banks):
                    pe.wait_ge(rl_done, t - len(r_banks) + 1)
                elif t < NB:
                    pe.wait_ge(sl_copied, t + 1)
                pe.wait_ge(xl_done, t // IT + 1)
                x_products(r_banks[t % len(r_banks)][:], t).then_inc(r_done, 1)
                if t == S6_AFTER:
                    pe.wait_ge(w6_split, 1)
                    pe.wait_ge(xl_done, NB)
                    for m in range(JT):
                        ins = small_products(m)
                    ins.then_inc(s6_done, 1)
            pe.wait_ge(r_cols, 2)
            pe.wait_ge(s6_copied, 2)
            pe.sem_inc(gcn_out, IT)
            pe.sem_inc(att_out, IT)

            last = NB - 1

            def adj_part(b, jt, it):
                a = adj[:, bass.ds((b * JT + jt) * IB + it * P, P)]
                if jt == 0:
                    pe.wait_ge(gcn_out, b * IT + it + 1)
                nc.tensor.matmul(gcn[it][:, 0:GC], a, r_hi[:, jt, G0:RC], start=(jt == 0), stop=False,
                                 skip_group_check=True)
                return nc.tensor.matmul(gcn[it][:, 0:GC], a, r_lo[:, jt, G0:RC], start=False,
                                        stop=(jt == JT - 1), skip_group_check=True)

            def high_part(b, jt, it):
                f = f_hi[:, jt % ST, it * P:(it + 1) * P]
                if jt == 0:
                    pe.wait_ge(rl_done, JT - IT + it + 1)
                    pe.wait_ge(att_out, b * IT + it + 1)
                nc.tensor.matmul(att[it][:, 0:HC], f, r_hi[:, jt, 0:HC], start=(jt == 0), stop=False,
                                 skip_group_check=True)
                nc.tensor.matmul(att[it][:, 0:D], f, r_lo[:, jt, 0:D], start=False, stop=False,
                                 skip_group_check=True)

            def low_part(b, jt, it):
                ins = nc.tensor.matmul(att[it][:, 0:HC], f_lo[:, jt % ST, it * P:(it + 1) * P],
                                       r_hi[:, jt, 0:HC], start=False, stop=(jt == JT - 1),
                                       skip_group_check=True)
                if jt == JT - 1 and (it < IT - 1 or b is last):
                    ins.then_inc(sums_done, 1)
                return ins

            def unit(b, jt):
                pe.wait_ge(rl_done, max(jt + 1, JT - IT))
                if jt % GJ == 0:
                    pe.wait_ge(adj_ready, b * NG + jt // GJ + 1)
                if jt in (0, JT - 1):
                    for it in range(IT):
                        adj_part(b, jt, it)
                        if it == 0:
                            pe.wait_ge(fh_done, b * (JT // 2) + jt // 2 + 1)
                            pe.wait_ge(fl_done, b * (JT // 2) + jt // 2 + 1)
                        high_part(b, jt, it)
                        ins = low_part(b, jt, it)
                else:
                    for it in range(IT):
                        adj_part(b, jt, it)
                    pe.wait_ge(fh_done, b * (JT // 2) + jt // 2 + 1)
                    for it in range(IT):
                        high_part(b, jt, it)
                    pe.wait_ge(fl_done, b * (JT // 2) + jt // 2 + 1)
                    for it in range(IT):
                        ins = low_part(b, jt, it)
                return ins

            with pe.Fori(0, NB - 1) as b:
                for jt in range(JT):
                    unit(b, jt).then_inc(unit_used, 1)
            for jt in range(JT - TAIL):
                unit(last, jt).then_inc(unit_used, 1)
            pe.wait_ge(adj_ready, NB * NG)

            def tail_adj(it):
                for jt in range(JT - TAIL, JT):
                    ins = adj_part(last, jt, it)
                ins.then_inc(gcn_sums, 1)

            tail_adj(0)
            for it in range(IT):
                if it + 1 < IT - 1:
                    tail_adj(it + 1)
                if it == IT - 1:
                    tail_adj(it)
                for jt in range(JT - TAIL, JT):
                    if it == 0:
                        pe.wait_ge(fh_done, (last * JT + jt) // 2 + 1)
                    high_part(last, jt, it)
                    if it == 0:
                        pe.wait_ge(fl_done, (last * JT + jt) // 2 + 1)
                    low_part(last, jt, it)


def kernel(x, adj, L0_gnn_W_sa, L0_gnn_a_sa, L0_gnn_W_gcnb, L0_gnn_b_gcnb, L0_gnn_Wa, L0_gnn_ba, L0_gnn_Wb,
           L0_gnn_bb):
    import numpy as np
    import concourse.bacc as bacc
    from concourse.bass_utils import run_bass_kernel_spmd

    x, adj = np.asarray(x), np.asarray(adj)
    w_sa, w_g = np.asarray(L0_gnn_W_sa), np.asarray(L0_gnn_W_gcnb)
    a_sa, wa, wb = np.asarray(L0_gnn_a_sa)[0], np.asarray(L0_gnn_Wa)[0], np.asarray(L0_gnn_Wb)[0]

    def rows(m):
        return np.ascontiguousarray(m.reshape(-1, P, m.shape[-1]).transpose(1, 0, 2))

    arrays = {
        "in_xT": rows(np.ascontiguousarray(x.T)),
        "in_xrows": rows(x),
        "in_adjT": np.ascontiguousarray(
            adj.T.reshape(JT, P, NB, IB).transpose(1, 2, 0, 3).reshape(P, NB * JT * IB)),
        "in_w": rows(np.concatenate([w_sa, w_g], axis=1)),
        "in_w_small": rows(np.stack([wa[:D], wb[:D], wa[D:], wb[D:]], axis=1)),
        "in_w_saT": rows(np.ascontiguousarray(w_sa.T)),
        "in_a_cols": rows(np.stack([a_sa[:D], a_sa[D:]], axis=1)),
        "in_b_row": np.ascontiguousarray(np.asarray(L0_gnn_b_gcnb)),
        "in_gate_bias": np.concatenate([np.asarray(L0_gnn_ba), np.asarray(L0_gnn_bb)]),
        "in_exponent": np.full((IT,), -0.5, np.float32),
    }
    nc = bacc.Bacc("TRN2", target_bir_lowering=False, num_devices=1)
    args = [nc.dram_tensor(name, a.shape, mybir.dt.from_np(a.dtype), kind="ExternalInput").ap()
            for name, a in arrays.items()]
    out = nc.dram_tensor("out_dram", (P, JT, D), F32, kind="ExternalOutput").ap()
    graph_layer(nc, *args, out)
    r = run_bass_kernel_spmd(nc, [arrays], core_ids=[0])
    got = r.results[0]["out_dram"]
    return np.ascontiguousarray(got.transpose(1, 0, 2).reshape(N, D))
```
